# Optimizing a Trainium2 kernel written in Bass

```python
import numpy as np
import jax
import jax.numpy as jnp

def _softmax(x, axis=-1):
    return jax.nn.softmax(x, axis=axis)

def _gelu(x):
    return jax.nn.gelu(x, approximate=True)

def _silu(x):
    return jax.nn.silu(x)

def _sigmoid(x):
    return jax.nn.sigmoid(x)

def _layernorm(x, axis=-1, eps=1e-05):
    m = jnp.mean(x, axis=axis, keepdims=True)
    v = jnp.var(x, axis=axis, keepdims=True)
    return (x - m) / jnp.sqrt(v + eps)

def _scatter_add(tgt, idx, src, axis=0):
    return tgt.at[idx].add(src)

def _segment_sum(src, seg, n):
    return jax.ops.segment_sum(src, seg, n)
kernel_name = 'mk_xattn_ffn_d1_seqx_r4_c6ec25'

def setup_inputs(seed: int=0):
    np.random.seed(seed)
    _w = jnp.asarray

    def _rec_inputs():
        import jax
        import jax.numpy as jnp
        _rk = jax.random.key(seed)
        x = -0.000125 + 0.9999 * jax.random.normal(jax.random.fold_in(_rk, 1), (16, 128, 256), jnp.float32)
        _lenS = 128 - jax.random.randint(jax.random.fold_in(_rk, 7), (16,), 0, max(1, 128 // 4) + 1, jnp.int32)
        _lenS2 = 128 - jax.random.randint(jax.random.fold_in(_rk, 8), (16,), 0, max(1, 128 // 4) + 1, jnp.int32)
        _ctx_1024P = jax.random.normal(jax.random.fold_in(_rk, 11), (16, 16, 256), jnp.float32)
        _ctx_1024c = jax.random.dirichlet(jax.random.fold_in(_rk, 511), 0.3 * jnp.ones((16,), jnp.float32), (16, 128))
        _ctx_1024t = jnp.einsum('bsk,bkd->bsd', _ctx_1024c, _ctx_1024P)
        _ctx_1024t = _ctx_1024t * jax.lax.rsqrt(jnp.mean(jnp.square(_ctx_1024t)) + 1e-12) * 0.953939
        ctx_1024 = -1.52775e-05 + 0.999936 * (_ctx_1024t + 0.3 * jax.random.normal(jax.random.fold_in(_rk, 611), (16, 128, 256), jnp.float32))
        return (x, ctx_1024)
    x, ctx_1024 = _rec_inputs()

    def _L0_xattn_setup():
        import jax, jax.numpy as jnp
        import numpy as np
        N_HEADS = 4
        IN_FEATURES = 256

        def _channel_attention(qm, km, vm, scale):
            b, n, c = qm.shape
            d = c // N_HEADS
            qh = qm.reshape(b, n, N_HEADS, d).transpose(0, 2, 3, 1)
            kh = km.reshape(b, n, N_HEADS, d).transpose(0, 2, 3, 1)
            vh = vm.reshape(b, n, N_HEADS, d).transpose(0, 2, 3, 1)
            scores = jnp.einsum('bhdn,bhen->bhde', qh, kh) * scale
            attn = jax.nn.softmax(scores, axis=-1)
            out = jnp.einsum('bhde,bhen->bhdn', attn, vh)
            return out.transpose(0, 3, 1, 2).reshape(b, n, c)
        key = jax.random.key(seed)
        ks = jax.random.split(key, 20)
        B, HW, C = (2, 4096, 256)
        inp = {'q': jax.random.normal(ks[0], (B, HW, C), dtype=jnp.float32), 'k': jax.random.normal(ks[1], (B, HW, C), dtype=jnp.float32), 'v': jax.random.normal(ks[2], (B, HW, C), dtype=jnp.float32)}
        names = ['wqg', 'bqg', 'wkg', 'bkg', 'wvg', 'bvg', 'wql', 'bql', 'wkl', 'bkl', 'wvl', 'bvl', 'wp', 'bp']
        for i, n in enumerate(names):
            inp[n] = jax.random.normal(ks[3 + i], (C,), dtype=jnp.float32)
        return inp
    _L0_xattn_all = _L0_xattn_setup()
    _L0_xattn_in = {k: v for k, v in _L0_xattn_all.items() if k in ('wqg', 'bqg', 'wkg', 'bkg', 'wvg', 'bvg', 'wql', 'bql', 'wkl', 'bkl', 'wvl', 'bvl', 'wp', 'bp')}
    del _L0_xattn_all

    def _L0_ffn_setup():
        import jax, jax.numpy as jnp
        import numpy as np
        B, S, D, E, F, TOP_K = (4, 512, 256, 8, 1024, 2)
        key = jax.random.key(seed)
        k0, k1, k2, k3 = jax.random.split(key, 4)
        init = lambda k, shape, fan: (jax.random.normal(k, shape, jnp.float32) / np.sqrt(fan)).astype(jnp.float32)
        return {'x': jax.random.normal(k0, (B, S, D), jnp.float32), 'gate_w': init(k1, (D, E), D), 'w1': init(k2, (E, D, F), D), 'b1': jnp.zeros((E, F), jnp.float32), 'w2': init(k3, (E, F, D), F), 'b2': jnp.zeros((E, D), jnp.float32)}
    _L0_ffn_all = _L0_ffn_setup()
    _L0_ffn_in = {k: v for k, v in _L0_ffn_all.items() if k in ('gate_w', 'w1', 'b1', 'w2', 'b2')}
    del _L0_ffn_all
    return {'x': x, 'ctx_1024': ctx_1024, 'L0_xattn_wqg': _L0_xattn_in['wqg'], 'L0_xattn_bqg': _L0_xattn_in['bqg'], 'L0_xattn_wkg': _L0_xattn_in['wkg'], 'L0_xattn_bkg': _L0_xattn_in['bkg'], 'L0_xattn_wvg': _L0_xattn_in['wvg'], 'L0_xattn_bvg': _L0_xattn_in['bvg'], 'L0_xattn_wql': _L0_xattn_in['wql'], 'L0_xattn_bql': _L0_xattn_in['bql'], 'L0_xattn_wkl': _L0_xattn_in['wkl'], 'L0_xattn_bkl': _L0_xattn_in['bkl'], 'L0_xattn_wvl': _L0_xattn_in['wvl'], 'L0_xattn_bvl': _L0_xattn_in['bvl'], 'L0_xattn_wp': _L0_xattn_in['wp'], 'L0_xattn_bp': _L0_xattn_in['bp'], 'L0_ffn_gate_w': _L0_ffn_in['gate_w'], 'L0_ffn_w1': _L0_ffn_in['w1'], 'L0_ffn_b1': _L0_ffn_in['b1'], 'L0_ffn_w2': _L0_ffn_in['w2'], 'L0_ffn_b2': _L0_ffn_in['b2']}

def reference(x, ctx_1024, L0_xattn_wqg, L0_xattn_bqg, L0_xattn_wkg, L0_xattn_bkg, L0_xattn_wvg, L0_xattn_bvg, L0_xattn_wql, L0_xattn_bql, L0_xattn_wkl, L0_xattn_bkl, L0_xattn_wvl, L0_xattn_bvl, L0_xattn_wp, L0_xattn_bp, L0_ffn_gate_w, L0_ffn_w1, L0_ffn_b1, L0_ffn_w2, L0_ffn_b2):
    import jax
    import jax.numpy as jnp

    def _L0_xattn_ref(q, k, v, wqg, bqg, wkg, bkg, wvg, bvg, wql, bql, wkl, bkl, wvl, bvl, wp, bp):
        import jax, jax.numpy as jnp
        import numpy as np
        N_HEADS = 4
        IN_FEATURES = 256

        def _channel_attention(qm, km, vm, scale):
            b, n, c = qm.shape
            d = c // N_HEADS
            qh = qm.reshape(b, n, N_HEADS, d).transpose(0, 2, 3, 1)
            kh = km.reshape(b, n, N_HEADS, d).transpose(0, 2, 3, 1)
            vh = vm.reshape(b, n, N_HEADS, d).transpose(0, 2, 3, 1)
            scores = jnp.einsum('bhdn,bhen->bhde', qh, kh) * scale
            attn = jax.nn.softmax(scores, axis=-1)
            out = jnp.einsum('bhde,bhen->bhdn', attn, vh)
            return out.transpose(0, 3, 1, 2).reshape(b, n, c)
        scale = IN_FEATURES ** (-0.5)
        att_global = _channel_attention(q * wqg + bqg, k * wkg + bkg, v * wvg + bvg, scale)
        att_local = _channel_attention(q * wql + bql, k * wkl + bkl, v * wvl + bvl, scale)
        att = att_global + att_local
        return 2.0 * att * wp + bp

    def _L0_ffn_ref(x, gate_w, w1, b1, w2, b2):
        import jax, jax.numpy as jnp
        import numpy as np
        B, S, D, E, F, TOP_K = (4, 512, 256, 8, 1024, 2)
        b, s, d = x.shape
        e = gate_w.shape[1]
        xf = x.reshape(-1, d)
        t = xf.shape[0]
        logits = xf @ gate_w
        top_w, top_idx = jax.lax.top_k(logits, TOP_K)
        top_w = jax.nn.softmax(top_w.astype(jnp.float32), axis=-1).astype(x.dtype)
        combine = jnp.zeros((t, e), x.dtype).at[jnp.arange(t)[:, None], top_idx].add(top_w)
        h = jax.nn.gelu(jnp.einsum('td,edf->tef', xf, w1) + b1, approximate=False)
        y = jnp.einsum('tef,efd->ted', h, w2) + b2
        out = jnp.einsum('ted,te->td', y, combine)
        return out.reshape(b, s, d)
    x = x + _L0_xattn_ref(_layernorm(x, axis=-1), ctx_1024, ctx_1024, L0_xattn_wqg, L0_xattn_bqg, L0_xattn_wkg, L0_xattn_bkg, L0_xattn_wvg, L0_xattn_bvg, L0_xattn_wql, L0_xattn_bql, L0_xattn_wkl, L0_xattn_bkl, L0_xattn_wvl, L0_xattn_bvl, L0_xattn_wp, L0_xattn_bp)
    x = x + _L0_ffn_ref(_layernorm(x, axis=-1), L0_ffn_gate_w, L0_ffn_w1, L0_ffn_b1, L0_ffn_w2, L0_ffn_b2)
    return x

_drawn_inputs = setup_inputs


def setup_inputs(seed=0):
    import zlib

    import numpy as np

    out = dict(_drawn_inputs(seed))
    spreads = {'L0_ffn_b1': (0.0, 0.596), 'L0_ffn_b2': (0.0, 0.423)}
    factors = {}
    for name, (base, spread) in spreads.items():
        noise = np.random.default_rng([zlib.crc32(name.encode()), seed]).standard_normal(out[name].shape)
        drawn = base * np.exp(spread * noise) if base else spread * noise
        out[name] = jnp.asarray(drawn.astype(out[name].dtype))
    for name, factor in factors.items():
        out[name] = (out[name] * factor).astype(out[name].dtype)
    return out
```

```python
from contextlib import ExitStack

import concourse.bass as bass
from concourse import mybir

ALU = mybir.AluOpType
ACT = mybir.ActivationFunctionType
AX = mybir.AxisListType
F32 = mybir.dt.float32
I32 = mybir.dt.int32

P = 128
EPS = 1e-5
BIG = 3.0e38


def after(eng, sem, value):
    if not isinstance(value, int) or value > 0:
        eng.wait_ge(sem, value)


def run_steps(eng, first, last, steady_from, steady_to, step):
    for i in range(first, steady_from):
        step(i, i)
    pairs = (steady_to - steady_from) // 2
    with eng.Fori(0, pairs) as pair:
        for u in range(2):
            step(pair * 2 + (steady_from + u), steady_from + u)
    for i in range(steady_from + 2 * pairs, last):
        step(i, i)


def xattn_moe_kernel(nc, x, ctx_in, wqg, bqg, wkg, bkg, wvg, bvg, wql, bql, wkl, bkl, wvl, bvl, wp, bp,
                     gate_w, w1, b1, w2, b2, out):
    T, _, D = x.shape
    E, _, F = w1.shape
    C = D // P
    FC = F // P
    HD = D // 4
    TOKENS = T * P
    NB = 2 * TOKENS // P + E - 1
    ROWS = TOKENS + P
    SCALE = float(D) ** -0.5
    GROUPS = 4
    TG = T // GROUPS

    xn_dram = nc.dram_tensor("xn_rows", (ROWS, D), F32, kind="Internal").ap()
    acc_dram = nc.dram_tensor("acc_rows", (ROWS, D), F32, kind="Internal").ap()
    out_rows = out.rearrange("b s d -> (b s) d")

    with ExitStack() as ctx:
        def sb(name, shape, dt=F32):
            return ctx.enter_context(nc.sbuf_tensor(name, shape, dt))

        def sem(name):
            return ctx.enter_context(nc.semaphore(name))

        W1 = sb("W1", [P, E, C, F])
        W2 = sb("W2", [P, E, FC, D])
        X = sb("X", [P, T, D])
        CX = sb("CX", [P, 2, D])
        def carver(whole):
            used = [0]

            def piece(*shape):
                n = 1
                for s in shape:
                    n *= s
                a = whole[:, used[0]:used[0] + n]
                used[0] += n
                names = "abcd"[:len(shape)]
                return a.rearrange(f"p ({' '.join(names)}) -> p {' '.join(names)}", **dict(zip(names, shape)))

            return piece

        shared = sb("shared", [P, 30 * D])
        att = carver(shared)
        rout = carver(shared)
        exs = carver(shared)
        QW = att(2, D)
        QB = att(2, D)
        KW = att(2, D)
        KB = att(2, D)
        BP = att(D)
        ident = sb("ident", [P, P])
        ones = sb("ones", [P, P])
        tri = sb("tri", [P, P])
        vrows = sb("vrows", [10, P])
        vcols = sb("vcols", [P, 10])
        b1rows = sb("b1rows", [E * FC, P])
        b1T = sb("b1T", [P, E * FC])
        GW = sb("GW", [P, C, E])
        half = sb("half", [P, 1])
        eps = sb("eps", [P, 1])
        st6 = sb("st6", [P, 2, 6])
        mv1 = sb("mv1", [P, 2, 2])
        rs1 = sb("rs1", [P, 2])
        mv2 = sb("mv2", [P, 2, 2])
        rs2 = sb("rs2", [P, 2])
        qu = att(2, D)
        q = att(2, 2, D)
        k = att(2, 2, D)
        nmax = sb("nmax", [P, 2, 4])
        ex = att(2, 4, HD)
        rsum = sb("rsum", [P, 2, 4])
        rinv = sb("rinv", [P, 2, 4])
        rw = sb("rw", [P, 2, 4])
        bd = sb("bd", [P, 2, 4, P])
        aT = att(4, P)
        vT = att(2, 4, P)
        xn = sb("xn", [P, 2, D])
        xnT = sb("xnT", [P, C, P])
        L = sb("L", [P, T, E])
        iotaE = sb("iotaE", [P, E])
        iotaB = sb("iotaB", [P, NB])
        iotaR = sb("iotaR", [P, P])
        tokid = sb("tokid", [P, T])
        slotno = sb("slotno", [P, 1])
        segm = sb("segm", [P, E, T])
        m12 = sb("m12", [P, 2, T])
        mask = rout(2, T * E)
        mk = [mask[:, n, :].rearrange("p (t e) -> p t e", e=E) for n in range(2)]
        tmpA = rout(T, E)
        tmpB = rout(T, E)
        tmpC = rout(E, T)
        tmpD = rout(E, T)
        tot = rout(E, T)
        sel = rout(T)
        ew = rout(T)
        den = rout(T)
        wk2 = sb("wk2", [P, 2, T])
        posf = sb("posf", [P, 2, T])
        posi = sb("posi", [P, 2, T], I32)
        slot_i = sb("slot_i", [P, 2, T], I32)
        blk_i = sb("blk_i", [P, 2, T], I32)
        slot_f = sb("slot_f", [P, 2, T])
        blk_f = sb("blk_f", [P, 2, T])
        cnt_i = sb("cnt_i", [P, E], I32)
        cnt_s = sb("cnt_s", [P, E], I32)
        nblk = sb("nblk", [P, E])
        cblk = sb("cblk", [P, E])
        offs = sb("offs", [P, E])
        onesE = sb("onesE", [P, E])
        cmpb = rout(NB, E)
        ebf = sb("ebf", [P, NB])
        expert = sb("expert", [P, NB], I32)
        ohB = rout(2 * T, NB)
        V = rout(2 * T, 2 * NB)
        ohR = rout(4, P)
        tv = sb("tv", [P, NB])
        tw = sb("tw", [P, NB])
        row_of = sb("row_of", [P, NB], I32)
        w_of = sb("w_of", [P, NB])
        gix = sb("gix", [P, 2], I32)
        six = sb("six", [P, 2], I32)
        XG = exs(2, D)
        XT = exs(2, C, P)
        hp = exs(F)
        hb = exs(FC, P)
        hT = exs(2, FC, P)
        Y = exs(2, D)
        B2 = exs(E, D)

        ps = [ctx.enter_context(nc.psum_tensor(f"bank{n}", [P, 512], F32)) for n in range(8)]
        pS = [ps[n][:, 0:4 * HD].rearrange("p (a e) -> p a e", e=HD) for n in range(2)]
        pCT = ps[2][:, 0:D].rearrange("p (c n) -> p c n", c=C)
        pAT = ps[3][:, :].rearrange("p (a d) -> p a d", d=P)
        pO = ps[4][:, 0:D]
        pXT = ps[5][:, 0:D].rearrange("p (c n) -> p c n", c=C)
        pL = ps[6][:, 0:T * E].rearrange("p (t e) -> p t e", e=E)
        pMisc = ps[7]
        pTok = ps[6][:, 0:2 * NB]
        pH = [ps[0], ps[1]]
        pHT = [ps[2][:, :].rearrange("p (c n) -> p c n", n=P), ps[3][:, :].rearrange("p (c n) -> p c n", n=P)]
        pY = [ps[4][:, 0:D], ps[5][:, 0:D]]
        pGT = ps[6][:, 0:D].rearrange("p (c n) -> p c n", c=C)

        x_in = [sem(f"x_in{g}") for g in range(GROUPS)]
        c_in = [sem(f"c_in{n}") for n in range(2)]
        kc_in, qc_in, v_in, w_in = sem("kc_in"), sem("qc_in"), sem("v_in"), sem("w_in")
        b2_in = sem("b2_in")
        zero_out = sem("zero_out")
        xn_out = [sem(f"xn_out{n}") for n in range(2)]
        x1_out = sem("x1_out")
        acc_in = [sem(f"acc_in{g}") for g in range(GROUPS)]
        res_out = sem("res_out")
        made = sem("made")
        zeroed = sem("zeroed")
        kscaled = sem("kscaled")
        vtr, vcopied = sem("vtr"), sem("vcopied")
        st1a, st1, rs1a, rs1_ok = sem("st1a"), sem("st1"), sem("rs1a"), sem("rs1_ok")
        qmul, q_ok, kmul, k_ok, xb_ok = sem("qmul"), sem("q_ok"), sem("kmul"), sem("k_ok"), sem("xb_ok")
        s_ok, max_ok, exp_ok, inv_ok, rw_ok, bd_ok = (sem("s_ok"), sem("max_ok"), sem("exp_ok"), sem("inv_ok"),
                                                      sem("rw_ok"), sem("bd_ok"))
        ct_ok, vt_ok, at_ok, as_ok, o_ok = sem("ct_ok"), sem("vt_ok"), sem("at_ok"), sem("as_ok"), sem("o_ok")
        x1_ok, st2a, st2, rs2a, rs2_ok, xn_ok = (sem("x1_ok"), sem("st2a"), sem("st2"), sem("rs2a"), sem("rs2_ok"),
                                                 sem("xn_ok"))
        xt_ok, xts_ok, l_ok = sem("xt_ok"), sem("xts_ok"), sem("l_ok")
        waited_pool, waited_dve = sem("waited_pool"), sem("waited_dve")
        route = sem("route")
        gap_ok, gate_exp = sem("gap_ok"), sem("gate_exp")
        mask_ok, rank_ok = sem("mask_ok"), sem("rank_ok")
        ohr_ok, table_mm, tok_ok = sem("ohr_ok"), sem("table_mm"), sem("tok_ok")
        gix_ok, six_ok = sem("gix_ok"), sem("six_ok")
        xg_ok = [sem(f"xg_ok{n}") for n in range(2)]
        gt_ok, gts_ok, h_ok, hp_ok, ht_ok, hb_ok, gelu_ok, y_ok, ys_ok, added = (
            sem("gt_ok"), sem("gts_ok"), sem("h_ok"), sem("hp_ok"), sem("ht_ok"), sem("hb_ok"), sem("gelu_ok"),
            sem("y_ok"), sem("ys_ok"), sem("added"))

        MADE = 12
        A_FIRST, A_LAST = -2, T + 5
        A_FROM, A_TO = 4, T - 3
        B_LAST = NB + 3
        B_FROM, B_TO = 3, NB - 2
        B_TO -= (B_TO - B_FROM) % 2
        A_TO -= (A_TO - A_FROM) % 2

        def tile_on(i):
            return not isinstance(i, int) or 0 <= i < T

        def block_on(i):
            return not isinstance(i, int) or 0 <= i < NB

        def group_loaded(eng, sems, t):
            if isinstance(t, int):
                eng.wait_ge(sems[t // TG], 16)
            else:
                for s in sems:
                    eng.wait_ge(s, 16)

        block = ctx.enter_context(nc.Block())

        @block.sync
        def _(sp):
            def row(a):
                return a.partition_broadcast(P)

            def load_group(dst, src, g, s):
                sp.dma_start(dst[:, g * TG:(g + 1) * TG, :],
                             src[g * TG:(g + 1) * TG].rearrange("t p d -> p t d")).then_inc(s, 16)

            load_group(X, x, 0, x_in[0])

            def load_ctx(t, n):
                sp.dma_start(CX[:, n, :], ctx_in[bass.ds(t, 1)].rearrange("a p d -> p (a d)")).then_inc(c_in[n], 16)

            for t in range(2):
                load_ctx(t, t)
            for dst, srcs in ((KW, (wkg, wkl)), (KB, (bkg, bkl))):
                for n, src in enumerate(srcs):
                    sp.dma_start(dst[:, n, :], row(src)).then_inc(kc_in, 16)
            for dst, srcs in ((QW, (wqg, wql)), (QB, (bqg, bql))):
                for n, src in enumerate(srcs):
                    sp.dma_start(dst[:, n, :], row(src)).then_inc(qc_in, 16)
            sp.dma_start(BP[:, :], row(bp)).then_inc(qc_in, 16)
            for n, src in enumerate((wvg, bvg, wvl, bvl, wp)):
                sp.dma_start(vrows[2 * n:2 * n + 2, :], src.rearrange("(c p) -> c p", p=P)).then_inc(v_in, 16)
            sp.dma_start(b1rows[:, :], b1.rearrange("e (c p) -> (e c) p", p=P)).then_inc(v_in, 16)
            sp.dma_start(GW[:, :, :], gate_w.rearrange("(c p) e -> p c e", p=P)).then_inc(v_in, 16)
            for g in range(1, GROUPS):
                load_group(X, x, g, x_in[g])
            sp.wait_ge(zeroed, 1)
            sp.dma_start(xn_dram[TOKENS:ROWS, :], bd[:, 0, 0:2, :].rearrange("p a d -> p (a d)")).then_inc(zero_out, 16)
            sp.dma_start(acc_dram[TOKENS:ROWS, :], bd[:, 0, 2:4, :].rearrange("p a d -> p (a d)")).then_inc(zero_out, 16)

            def tiles(i, u):
                t = i + 3
                if tile_on(t) and not (isinstance(t, int) and t < 2):
                    sp.wait_ge(k_ok, t - 1)
                    sp.wait_ge(ct_ok, t - 1)
                    load_ctx(t, (u + 3) % 2)
                t = i - 1
                if not tile_on(t):
                    return
                sp.wait_ge(x1_ok, t + 1)
                sp.dma_start(acc_dram[bass.ds(t * P, P), :], X[:, bass.ds(t, 1), :].rearrange("p a d -> p (a d)"))\
                  .then_inc(x1_out, 16)
                sp.wait_ge(xn_ok, t + 1)
                n = (u - 1) % 2
                sp.dma_start(xn_dram[bass.ds(t * P, P), :], xn[:, n, :]).then_inc(xn_out[n], 16)

            run_steps(sp, -1, T + 1, A_FROM, A_TO, tiles)

            sp.wait_ge(tok_ok, 2)
            sp.dma_start(B2[0:1, :, :], b2.rearrange("(a e) d -> a e d", a=1)).then_inc(b2_in, 16)

            sp.wait_ge(added, 16 * NB)
            for g in range(GROUPS):
                rows = slice(g * TG * P, (g + 1) * TG * P)
                sp.dma_start(X[:, g * TG:(g + 1) * TG, :], acc_dram[rows, :].rearrange("(t p) d -> p t d", p=P))\
                  .then_inc(acc_in[g], 16)
            for g in range(GROUPS):
                rows = slice(g * TG * P, (g + 1) * TG * P)
                sp.wait_ge(acc_in[g], 16)
                sp.dma_start(out_rows[rows, :].rearrange("(t p) d -> p t d", p=P), X[:, g * TG:(g + 1) * TG, :])\
                  .then_inc(res_out, 16)
            sp.wait_ge(res_out, 16 * GROUPS)

        @block.gpsimd
        def _(pool):
            pool.memset(bd[:, :, :, :], 0.0).then_inc(zeroed, 1)
            pool.memset(half[:, :], -0.5).then_inc(made, 1)
            pool.memset(eps[:, :], EPS).then_inc(made, 1)
            pool.memset(ident[:, :], 0.0).then_inc(made, 1)
            pool.memset(ones[:, :], 1.0).then_inc(made, 1)
            pool.wait_ge(made, 4)
            pool.affine_select(out=ident[:, :], in_=ident[:, :], compare_op=ALU.not_equal, fill=1.0, base=0,
                               pattern=[[-1, P]], channel_multiplier=1).then_inc(made, 1)
            pool.affine_select(out=tri[:, :], in_=ones[:, :], compare_op=ALU.is_ge, fill=0.0, base=-1,
                               pattern=[[1, P]], channel_multiplier=-1).then_inc(made, 1)
            pool.iota(iotaE[:, :], pattern=[[1, E]], base=-E, channel_multiplier=0,
                      allow_small_or_imprecise_dtypes=True).then_inc(made, 1)
            pool.iota(iotaB[:, :], pattern=[[1, NB]], base=0, channel_multiplier=0,
                      allow_small_or_imprecise_dtypes=True).then_inc(made, 1)
            pool.iota(iotaR[:, :], pattern=[[1, P]], base=0, channel_multiplier=0,
                      allow_small_or_imprecise_dtypes=True).then_inc(made, 1)
            pool.iota(tokid[:, :], pattern=[[P, T]], base=-TOKENS, channel_multiplier=1,
                      allow_small_or_imprecise_dtypes=True).then_inc(made, 1)
            pool.iota(slotno[:, :], pattern=[[0, 1]], base=0, channel_multiplier=1,
                      allow_small_or_imprecise_dtypes=True).then_inc(made, 1)
            pool.memset(onesE[:, :], 1.0).then_inc(made, 1)
            pool.memset(segm[:, :, :], 1.0).then_inc(zeroed, 1)
            pool.wait_ge(zeroed, 2)
            pool.memset(segm[:, :, 0:1], 0.0).then_inc(zeroed, 1)
            pool.wait_ge(kc_in, 16 * 4)
            pool.tensor_scalar(KW[:, :, :], KW[:, :, :], SCALE, None, ALU.mult).then_inc(kscaled, 1)
            pool.tensor_scalar(KB[:, :, :], KB[:, :, :], SCALE, None, ALU.mult).then_inc(kscaled, 1)

            def attention(i, u):
                t, n = i + 2, u % 2
                if tile_on(t):
                    v, r = mv1[:, n, 1:2], rs1[:, n:n + 1]
                    after(pool, q_ok, t - 1)
                    pool.wait_ge(st1, t + 1)
                    pool.tensor_tensor(r, v, eps[:, :], ALU.add).then_inc(rs1a, 1)
                    pool.wait_ge(rs1a, t + 1)
                    pool.tensor_tensor(r, r, half[:, :], ALU.pow).then_inc(rs1_ok, 1)
                t, n = i + 1, (u + 1) % 2
                if tile_on(t):
                    pool.wait_ge(c_in[n], 8 * (t - n) + 16)
                    pool.wait_ge(kscaled, 2)
                    after(pool, s_ok, t - 1)
                    c = CX[:, n:n + 1, :].broadcast_to([P, 2, D])
                    pool.tensor_tensor(k[:, n], c, KW[:, :, :], ALU.mult).then_inc(kmul, 1)
                    pool.wait_ge(kmul, t + 1)
                    pool.tensor_tensor(k[:, n], k[:, n], KB[:, :, :], ALU.add).then_inc(k_ok, 1)
                t = i
                if tile_on(t):
                    xt = X[:, bass.ds(t, 1), :].rearrange("p a d -> p (a d)")
                    pool.wait_ge(q_ok, t + 1)
                    pool.wait_ge(qc_in, 16 * 5)
                    pool.tensor_tensor(xt, xt, BP[:, :], ALU.add).then_inc(xb_ok, 1)
                t, n = i - 1, (u - 1) % 2
                if tile_on(t):
                    v, r = mv2[:, n, 1:2], rs2[:, n:n + 1]
                    after(pool, xn_ok, t - 1)
                    pool.wait_ge(st2, t + 1)
                    pool.tensor_tensor(r, v, eps[:, :], ALU.add).then_inc(rs2a, 1)
                    pool.wait_ge(rs2a, t + 1)
                    pool.tensor_tensor(r, r, half[:, :], ALU.pow).then_inc(rs2_ok, 1)

            run_steps(pool, A_FIRST, A_LAST, A_FROM, A_TO, attention)

            pool.wait_ge(tok_ok, 2)
            pool.wait_ge(zero_out, 32)
            pool.wait_ge(xn_out[0], 16 * (T // 2))

            def experts(i, u):
                b, n = i + 2, u % 2
                if block_on(b):
                    after(pool, xg_ok[n], 8 * (b - n))
                    pool.tensor_copy(gix[:, n:n + 1], row_of[:, bass.ds(b, 1)]).then_inc(gix_ok, 1)
                    pool.wait_ge(xn_out[1], 16 * (T // 2))
                    pool.wait_ge(gix_ok, b + 1)
                    after(pool, gt_ok, b - 1)
                    pool.sem_inc(waited_pool, 1)
                    pool.indirect_dma_start(out=XG[:, n, :], out_offset=None, in_=xn_dram,
                                            in_offset=bass.IndirectOffsetOnAxis(ap=gix[:, n:n + 1], axis=0))\
                        .then_inc(xg_ok[n], 16)
                b, n = i - 3, (u - 3) % 2
                if block_on(b):
                    after(pool, added, 16 * b)
                    pool.tensor_copy(six[:, n:n + 1], row_of[:, bass.ds(b, 1)]).then_inc(six_ok, 1)
                    pool.wait_ge(x1_out, 16 * T)
                    pool.wait_ge(six_ok, b + 1)
                    pool.wait_ge(ys_ok, b + 1)
                    pool.sem_inc(waited_pool, 1)
                    pool.indirect_dma_start(out=acc_dram,
                                            out_offset=bass.IndirectOffsetOnAxis(ap=six[:, n:n + 1], axis=0),
                                            in_=Y[:, n, :], in_offset=None, compute_op=ALU.add,
                                            bounds_check=ROWS - 1, oob_is_err=True).then_inc(added, 16)

            run_steps(pool, -2, B_LAST, B_FROM, B_TO, experts)

        @block.scalar
        def _(act):
            for e in range(E):
                act.dma_start(W1[:, e], w1[e].rearrange("(c p) f -> p c f", p=P)).then_inc(w_in, 16)
                act.dma_start(W2[:, e], w2[e].rearrange("(c p) d -> p c d", p=P)).then_inc(w_in, 16)
            act.wait_ge(vtr, 2)
            act.activation(vcols[:, :], pMisc[:, 0:10], ACT.Copy).then_inc(vcopied, 1)
            act.activation(b1T[:, :], pMisc[:, 64:64 + E * FC], ACT.Copy).then_inc(vcopied, 1)
            act.wait_ge(vcopied, 2)
            act.activation(vcols[:, 8:10], vcols[:, 8:10], ACT.Copy, scale=2.0).then_inc(vcopied, 1)

            def attention(i, u):
                t = i - 1
                if tile_on(t):
                    act.wait_ge(at_ok, t + 1)
                    after(act, o_ok, t)
                    act.activation(aT[:, :, :], pAT, ACT.Copy).then_inc(as_ok, 1)
                t, n = i, u % 2
                if tile_on(t):
                    act.wait_ge(max_ok, t + 1)
                    after(act, bd_ok, 2 * (t - 1))
                    for a in range(4):
                        act.activation(ex[:, n, a, :], pS[n][:, a, :], ACT.Exp, bias=nmax[:, n, a:a + 1],
                                       accum_out=rsum[:, n, a:a + 1]).then_inc(exp_ok, 1)
                t, n = i, u % 2
                if tile_on(t):
                    act.wait_ge(ct_ok, t + 1)
                    after(act, o_ok, t - 1)
                    for g in range(2):
                        for c in range(C):
                            act.activation(vT[:, n, 2 * g + c, :], pCT[:, c, :], ACT.Identity,
                                           bias=vcols[:, 4 * g + 2 + c:4 * g + 3 + c],
                                           scale=vcols[:, 4 * g + c:4 * g + c + 1]).then_inc(vt_ok, 1)

            run_steps(act, A_FIRST, A_LAST, A_FROM, A_TO, attention)

            act.wait_ge(gap_ok, 1)
            act.activation(ew, sel, ACT.Exp).then_inc(gate_exp, 1)

            def experts(i, u):
                b = i
                if block_on(b):
                    after(act, ht_ok, b)
                    for m in range(2):
                        act.wait_ge(h_ok, 2 * b + (m + 1))
                        act.activation(hp[:, m * 512:(m + 1) * 512], pH[m][:, :], ACT.Copy).then_inc(hp_ok, 1)
                b, n = i - 1, (u - 1) % 2
                if block_on(b):
                    after(act, y_ok, b - 1)
                    for m in range(2):
                        act.wait_ge(hb_ok, 2 * b + (m + 1))
                        act.activation(hT[:, n, 4 * m:4 * m + 4, :], hb[:, 4 * m:4 * m + 4, :], ACT.Gelu)\
                           .then_inc(gelu_ok, 1)

            run_steps(act, 0, B_LAST, B_FROM, B_TO, experts)

        @block.vector
        def _(dve):
            dve.wait_ge(vcopied, 3)
            dve.wait_ge(zeroed, 3)

            def attention(i, u):
                t, n = i, u % 2
                if tile_on(t):
                    dve.wait_ge(s_ok, t + 1)
                    after(dve, exp_ok, 4 * (t - 1))
                    dve.tensor_reduce(nmax[:, n, :], pS[n], AX.X, ALU.max, negate=True).then_inc(max_ok, 1)
                t, n = i + 1, (u + 1) % 2
                if tile_on(t):
                    xb = X[:, bass.ds(t, 1), :].broadcast_to([P, 2, D])
                    dve.wait_ge(rs1_ok, t + 1)
                    dve.wait_ge(qc_in, 16 * 5)
                    after(dve, q_ok, t)
                    dve.scalar_tensor_tensor(out=qu[:, :, :], in0=xb, scalar=mv1[:, n, 0:1], in1=QW[:, :, :],
                                             op0=ALU.subtract, op1=ALU.mult).then_inc(qmul, 1)
                    after(dve, s_ok, t - 1)
                    dve.wait_ge(qmul, t + 1)
                    dve.scalar_tensor_tensor(out=q[:, n], in0=qu[:, :, :], scalar=rs1[:, n:n + 1],
                                             in1=QB[:, :, :], op0=ALU.mult, op1=ALU.add).then_inc(q_ok, 1)
                t, n = i + 2, u % 2
                if tile_on(t):
                    group_loaded(dve, x_in, t)
                    dve.bn_stats(st6[:, 0, :], X[:, bass.ds(t, 1), :].rearrange("p a d -> p (a d)")).then_inc(st1a, 1)
                    dve.wait_ge(st1a, t + 1)
                    after(dve, qmul, t - 1)
                    after(dve, rs1a, t - 1)
                    dve.sem_inc(waited_dve, 1)
                    dve.bn_aggr(mv1[:, n, :], st6[:, 0, :]).then_inc(st1, 1)
                t, n = i, u % 2
                if tile_on(t):
                    dve.wait_ge(exp_ok, 4 * (t + 1))
                    dve.reciprocal(rinv[:, n, :], rsum[:, n, :]).then_inc(inv_ok, 1)
                    dve.wait_ge(inv_ok, t + 1)
                    dve.tensor_tensor(rw[:, n, :].rearrange("p (g c) -> p g c", g=2),
                                      rinv[:, n, :].rearrange("p (g c) -> p g c", g=2),
                                      vcols[:, 8:10].rearrange("p (g c) -> p g c", g=1).broadcast_to([P, 2, C]),
                                      ALU.mult).then_inc(rw_ok, 1)
                    dve.wait_ge(rw_ok, t + 1)
                    after(dve, at_ok, t - 1)
                    dve.wait_ge(zero_out, 32)
                    for h in range(2):
                        p = slice(h * HD, (h + 1) * HD)
                        dve.tensor_tensor(bd[p, n, :, p], ex[p, n, :, :],
                                          rw[p, n, :].rearrange("p (a b) -> p a b", b=1).broadcast_to([HD, 4, HD]),
                                          ALU.mult).then_inc(bd_ok, 1)
                t, n = i - 1, (u - 1) % 2
                if tile_on(t):
                    xt = X[:, bass.ds(t, 1), :].rearrange("p a d -> p (a d)")
                    dve.wait_ge(xb_ok, t + 1)
                    dve.wait_ge(o_ok, t + 1)
                    dve.tensor_tensor(xt, pO, xt, ALU.add).then_inc(x1_ok, 1)
                    dve.wait_ge(x1_ok, t + 1)
                    dve.sem_inc(waited_dve, 1)
                    dve.bn_stats(st6[:, 1, :], xt).then_inc(st2a, 1)
                    dve.wait_ge(st2a, t + 1)
                    after(dve, xn_ok, t - 1)
                    dve.sem_inc(waited_dve, 1)
                    dve.bn_aggr(mv2[:, n, :], st6[:, 1, :]).then_inc(st2, 1)
                t, n = i - 2, (u - 2) % 2
                if tile_on(t):
                    dve.wait_ge(rs2_ok, t + 1)
                    after(dve, xn_out[n], 8 * (t - n))
                    after(dve, xt_ok, t - 1)
                    dve.tensor_scalar(xn[:, n, :], X[:, bass.ds(t, 1), :].rearrange("p a d -> p (a d)"),
                                      mv2[:, n, 0:1], rs2[:, n:n + 1], ALU.subtract, ALU.mult).then_inc(xn_ok, 1)
                t = i - 3
                if tile_on(t):
                    dve.wait_ge(xt_ok, t + 1)
                    after(dve, l_ok, t)
                    dve.tensor_copy(xnT[:, :, :], pXT).then_inc(xts_ok, 1)

            run_steps(dve, A_FIRST, A_LAST, A_FROM, A_TO, attention)

            steps = [0]

            def chain(ins):
                ins.then_inc(route, 1)
                steps[0] += 1
                dve.wait_ge(route, steps[0])

            def over_e(a):
                return a.rearrange("p (t o) -> p t o", o=1).broadcast_to([P, T, E])

            iota_te = iotaE[:, :].rearrange("p (o e) -> p o e", o=1).broadcast_to([P, T, E])
            dve.wait_ge(l_ok, T)
            dve.wait_ge(made, MADE)
            chain(dve.tensor_copy(L[:, :, :], pL))
            logits = L[:, :, :]
            for n in range(2):
                best = m12[:, n, :]
                chain(dve.tensor_reduce(best, logits, AX.X, ALU.max))
                chain(dve.tensor_tensor(tmpA, logits, over_e(best), ALU.is_equal))
                chain(dve.tensor_tensor(tmpA, tmpA, iota_te, ALU.mult))
                chain(dve.tensor_reduce(sel, tmpA, AX.X, ALU.min))
                chain(dve.tensor_tensor(mk[n], iota_te, over_e(sel), ALU.is_equal))
                if n == 0:
                    chain(dve.scalar_tensor_tensor(out=tmpB, in0=mk[0], scalar=-BIG, in1=logits,
                                                   op0=ALU.mult, op1=ALU.add))
                    logits = tmpB
            dve.tensor_tensor(tmpA, mk[0], mk[1], ALU.add).then_inc(mask_ok, 1)
            dve.tensor_tensor(sel, m12[:, 1, :], m12[:, 0, :], ALU.subtract).then_inc(gap_ok, 1)
            dve.wait_ge(gate_exp, 1)
            chain(dve.tensor_scalar(den, ew, 1.0, None, ALU.add))
            chain(dve.reciprocal(wk2[:, 0, :], den))
            chain(dve.tensor_tensor(wk2[:, 1, :], ew, wk2[:, 0, :], ALU.mult))
            dve.wait_ge(rank_ok, 1)
            pR = pMisc[:, 0:T * E].rearrange("p (t e) -> p t e", e=E)
            pTot = pMisc[:, T * E:2 * T * E].rearrange("p (t e) -> p e t", e=E)
            chain(dve.tensor_copy(tot, pTot))
            chain(dve.tensor_tensor_scan(tmpC.rearrange("p e t -> p (e t)"), segm[:, :, :].rearrange("p e t -> p (e t)"),
                                         tot.rearrange("p e t -> p (e t)"), 0.0, ALU.mult, ALU.add))
            last = tmpC[:, :, T - 1:T].rearrange("p e o -> p (e o)")
            chain(dve.tensor_scalar(cnt_i[:, :], last, float(P - 1), None, ALU.add))
            chain(dve.tensor_scalar(cnt_s[:, :], cnt_i[:, :], 7, None, ALU.arith_shift_right))
            chain(dve.tensor_copy(nblk[:, :], cnt_s[:, :]))
            chain(dve.tensor_tensor_scan(cblk[:, :], onesE[:, :], nblk[:, :], 0.0, ALU.mult, ALU.add))
            chain(dve.tensor_tensor(offs[:, :], cblk[:, :], nblk[:, :], ALU.subtract))
            chain(dve.tensor_scalar(offs[:, :], offs[:, :], float(P), None, ALU.mult))
            chain(dve.tensor_tensor(tmpD, tmpC, tot, ALU.subtract))
            chain(dve.tensor_tensor(tmpD, tmpD, offs[:, :].rearrange("p (e o) -> p e o", o=1).broadcast_to([P, E, T]),
                                    ALU.add))
            chain(dve.tensor_tensor(tmpA, pR, tmpD.rearrange("p e t -> p t e"), ALU.add))
            for n in range(2):
                chain(dve.tensor_tensor(tmpB, tmpA, mk[n], ALU.mult))
                chain(dve.tensor_reduce(posf[:, n, :], tmpB, AX.X, ALU.add))
            chain(dve.tensor_copy(posi[:, :, :], posf[:, :, :]))
            chain(dve.tensor_scalar(slot_i[:, :, :], posi[:, :, :], P - 1, None, ALU.bitwise_and))
            chain(dve.tensor_scalar(blk_i[:, :, :], posi[:, :, :], 7, None, ALU.arith_shift_right))
            chain(dve.tensor_copy(slot_f[:, :, :], slot_i[:, :, :]))
            chain(dve.tensor_copy(blk_f[:, :, :], blk_i[:, :, :]))
            chain(dve.tensor_tensor(cmpb, iotaB[:, :].rearrange("p (b o) -> p b o", o=1).broadcast_to([P, NB, E]),
                                    cblk[:, :].rearrange("p (o e) -> p o e", o=1).broadcast_to([P, NB, E]), ALU.is_ge))
            chain(dve.tensor_reduce(ebf[:, :], cmpb, AX.X, ALU.add))
            chain(dve.tensor_scalar(expert[:, :], ebf[:, :], float(E - 1), None, ALU.min))
            N2 = 2 * T

            def flat(a):
                return a.rearrange("p n (t o) -> p (n t) o", o=1).broadcast_to([P, N2, NB])

            chain(dve.tensor_tensor(ohB, iotaB[:, :].rearrange("p (o b) -> p o b", o=1).broadcast_to([P, N2, NB]),
                                    flat(blk_f[:, :, :]), ALU.is_equal))
            for n in range(2):
                dve.tensor_tensor(V[:, n * T:(n + 1) * T, 0:NB], ohB[:, n * T:(n + 1) * T, :],
                                  tokid[:, :].rearrange("p (t o) -> p t o", o=1).broadcast_to([P, T, NB]), ALU.mult)
            chain(dve.tensor_tensor(V[:, :, NB:2 * NB], ohB, flat(wk2[:, :, :]), ALU.mult))

            def slot_onehot(h):
                for r in range(4):
                    after(dve, table_mm, h * 4 + (r - 3) if not isinstance(h, int) else 4 * h + r - 3)
                    dve.tensor_scalar(ohR[:, r, :], iotaR[:, :],
                                      slot_f[:, :, :].rearrange("p n t -> p (n t)")[:, bass.ds(h * 4 + r, 1)],
                                      None, ALU.is_equal).then_inc(ohr_ok, 1)

            slot_onehot(0)
            with dve.Fori(1, N2 // 4) as h:
                slot_onehot(h)
            dve.wait_ge(table_mm, N2)
            chain(dve.tensor_scalar(tv[:, :], pTok[:, 0:NB], 0.0, None, ALU.is_ge))
            chain(dve.tensor_scalar(tw[:, :], pTok[:, 0:NB], float(TOKENS), None, ALU.add))
            chain(dve.tensor_scalar(tv[:, :], tv[:, :], slotno[:, 0:1], None, ALU.mult))
            dve.tensor_tensor(row_of[:, :], tw[:, :], tv[:, :], ALU.add).then_inc(tok_ok, 1)
            dve.tensor_copy(w_of[:, :], pTok[:, NB:2 * NB]).then_inc(tok_ok, 1)
            dve.wait_ge(tok_ok, 2)

            def experts(i, u):
                b, n = i + 1, (u + 1) % 2
                if block_on(b):
                    dve.wait_ge(gt_ok, b + 1)
                    after(dve, h_ok, 2 * (b - 1))
                    dve.tensor_copy(XT[:, n], pGT).then_inc(gts_ok, 1)
                b = i - 1
                if block_on(b):
                    e = dve.value_load(expert[0:1, bass.ds(b, 1)], min_val=0, max_val=E - 1)
                    for m in range(2):
                        dve.wait_ge(ht_ok, b + 1)
                        after(dve, gelu_ok, 2 * b + (m - 1) if not isinstance(b, int) else 2 * b + m - 1)
                        dve.tensor_tensor(hb[:, 4 * m:4 * m + 4, :], pHT[m],
                                          b1T[:, bass.ds(e * FC + 4 * m, 4)].rearrange("p (c o) -> p c o", o=1)
                                          .broadcast_to([P, 4, P]), ALU.add).then_inc(hb_ok, 1)
                b, n = i - 2, (u - 2) % 2
                if block_on(b):
                    dve.wait_ge(y_ok, b + 1)
                    after(dve, added, 16 * (b - 1))
                    dve.tensor_scalar(Y[:, n, :], pY[n], w_of[:, bass.ds(b, 1)], None, ALU.mult).then_inc(ys_ok, 1)

            run_steps(dve, -1, B_LAST, B_FROM, B_TO, experts)

        @block.tensor
        def _(pe):
            pe.wait_ge(made, MADE)
            pe.wait_ge(v_in, 16 * 7)
            pe.transpose(pMisc[:, 0:10], vrows[:, :], ident[0:10, 0:10]).then_inc(vtr, 1)
            pe.transpose(pMisc[:, 64:64 + E * FC], b1rows[:, :], ident[0:E * FC, 0:E * FC]).then_inc(vtr, 1)

            def attention(i, u):
                t, n = i - 1, (u - 1) % 2
                if tile_on(t):
                    pe.wait_ge(as_ok, t + 1)
                    pe.wait_ge(vt_ok, 4 * (t + 1))
                    after(pe, x1_ok, t)
                    for c in range(C):
                        for g in range(2):
                            mm = pe.matmul(pO[:, c * P:(c + 1) * P], vT[:, n, 2 * g + c, :], aT[:, 2 * g + c, :],
                                           start=(g == 0), stop=(g == 1))
                    mm.then_inc(o_ok, 1)
                t, n = i - 3, (u - 3) % 2
                if tile_on(t):
                    pe.wait_ge(xn_ok, t + 1)
                    after(pe, xts_ok, t)
                    for c in range(C):
                        mm = pe.transpose(pXT[:, c, :], xn[:, n, c * P:(c + 1) * P], ident[:, :])
                    mm.then_inc(xt_ok, 1)
                t, n = i + 1, (u + 1) % 2
                if tile_on(t):
                    pe.wait_ge(q_ok, t + 1)
                    pe.wait_ge(k_ok, t + 1)
                    after(pe, exp_ok, 4 * (t - 1))
                    for g in range(2):
                        for c in range(C):
                            for h in range(2):
                                ch = slice(c * P + h * HD, c * P + (h + 1) * HD)
                                mm = pe.matmul(pS[n][h * HD:(h + 1) * HD, 2 * g + c, :], q[:, n, g, ch], k[:, n, g, ch],
                                               start=True, stop=True)
                    mm.then_inc(s_ok, 1)
                t = i - 4
                if tile_on(t):
                    pe.wait_ge(xts_ok, t + 1)
                    for c in range(C):
                        mm = pe.matmul(pL[:, bass.ds(t, 1), :].rearrange("p a e -> p (a e)"), xnT[:, c, :], GW[:, c, :],
                                       start=(c == 0), stop=(c == C - 1))
                    mm.then_inc(l_ok, 1)
                t, n = i + 1, (u + 1) % 2
                if tile_on(t):
                    pe.wait_ge(c_in[n], 8 * (t - n) + 16)
                    after(pe, vt_ok, 4 * t)
                    for c in range(C):
                        mm = pe.transpose(pCT[:, c, :],
                                          CX[:, n, c * P:(c + 1) * P],
                                          ident[:, :])
                    mm.then_inc(ct_ok, 1)
                t, n = i, u % 2
                if tile_on(t):
                    pe.wait_ge(bd_ok, 2 * (t + 1))
                    after(pe, as_ok, t)
                    for a in range(4):
                        mm = pe.transpose(pAT[:, a, :], bd[:, n, a, :], ident[:, :])
                    mm.then_inc(at_ok, 1)

            run_steps(pe, A_FIRST, A_LAST, A_FROM, A_TO, attention)

            pe.wait_ge(mask_ok, 1)
            chosen = tmpA.rearrange("p t e -> p (t e)")
            pe.matmul(pMisc[:, 0:T * E], tri[:, :], chosen, start=True, stop=True)
            pe.matmul(pMisc[:, T * E:2 * T * E], ones[:, :], chosen, start=True, stop=True).then_inc(rank_ok, 1)

            def table(h, first, last):
                for r in range(4):
                    pe.wait_ge(ohr_ok, h * 4 + (r + 1))
                    pe.matmul(pTok, ohR[:, r, :],
                              V[:, bass.ds(h * 4 + r, 1), :].rearrange("p a b -> p (a b)"),
                              start=(first and r == 0), stop=(last and r == 3)).then_inc(table_mm, 1)

            N4 = 2 * T // 4
            table(0, True, False)
            with pe.Fori(1, N4 - 1) as h:
                table(h, False, False)
            table(N4 - 1, False, True)

            pe.wait_ge(w_in, 16 * 2 * E)
            pe.wait_ge(b2_in, 16)
            pe.wait_ge(tok_ok, 2)

            def experts(i, u):
                b, n = i + 1, (u + 1) % 2
                if block_on(b):
                    pe.wait_ge(xg_ok[n], 8 * (b + 2 - n))
                    after(pe, gts_ok, b)
                    for c in range(C):
                        mm = pe.transpose(pGT[:, c, :], XG[:, n, c * P:(c + 1) * P], ident[:, :])
                    mm.then_inc(gt_ok, 1)
                b, n = i, u % 2
                if block_on(b):
                    e = pe.value_load(expert[0:1, bass.ds(b, 1)], min_val=0, max_val=E - 1)
                    pe.wait_ge(gts_ok, b + 1)
                    for m in range(2):
                        after(pe, hp_ok, 2 * b + (m - 1) if not isinstance(b, int) else 2 * b + m - 1)
                        for c in range(C):
                            mm = pe.matmul(pH[m][:, :], XT[:, n, c, :],
                                           W1[:, bass.ds(e, 1), c, m * 512:(m + 1) * 512].rearrange("p a f -> p (a f)"),
                                           start=(c == 0), stop=(c == C - 1))
                        mm.then_inc(h_ok, 1)
                b = i - 1
                if block_on(b):
                    pe.wait_ge(hp_ok, 2 * (b + 1))
                    after(pe, hb_ok, 2 * b)
                    for f in range(FC):
                        mm = pe.transpose(pHT[f // 4][:, f % 4, :], hp[:, f * P:(f + 1) * P], ident[:, :])
                    mm.then_inc(ht_ok, 1)
                b, n = i - 2, (u - 2) % 2
                if block_on(b):
                    e = pe.value_load(expert[0:1, bass.ds(b, 1)], min_val=0, max_val=E - 1)
                    pe.wait_ge(gelu_ok, 2 * (b + 1))
                    after(pe, ys_ok, b - 1)
                    for f in range(FC):
                        pe.matmul(pY[n], hT[:, n, f, :], W2[:, bass.ds(e, 1), f, :].rearrange("p a d -> p (a d)"),
                                  start=(f == 0), stop=False)
                    pe.matmul(pY[n], ones[0:1, :], B2[0:1, bass.ds(e, 1), :].rearrange("p a d -> p (a d)"),
                              start=False, stop=True).then_inc(y_ok, 1)

            run_steps(pe, -1, B_LAST, B_FROM, B_TO, experts)


_INS = ["x", "ctx_1024", "L0_xattn_wqg", "L0_xattn_bqg", "L0_xattn_wkg", "L0_xattn_bkg", "L0_xattn_wvg", "L0_xattn_bvg",
        "L0_xattn_wql", "L0_xattn_bql", "L0_xattn_wkl", "L0_xattn_bkl", "L0_xattn_wvl", "L0_xattn_bvl", "L0_xattn_wp",
        "L0_xattn_bp", "L0_ffn_gate_w", "L0_ffn_w1", "L0_ffn_b1", "L0_ffn_w2", "L0_ffn_b2"]


def kernel(**inputs):
    import numpy as _np
    import concourse.bacc as _bacc
    from concourse import mybir as _mybir
    from concourse.bass_utils import run_bass_kernel_spmd as _run

    nc = _bacc.Bacc("TRN2", target_bir_lowering=False, num_devices=1)
    arrays, args = {}, []
    for name in _INS:
        a = _np.ascontiguousarray(inputs[name])
        arrays[f"in_{name}"] = a
        args.append(nc.dram_tensor(f"in_{name}", a.shape, _mybir.dt.from_np(a.dtype), kind="ExternalInput").ap())
    args.append(nc.dram_tensor("out_0", inputs["x"].shape, _mybir.dt.float32, kind="ExternalOutput").ap())
    xattn_moe_kernel(nc, *args)
    r = _run(nc, [arrays], core_ids=[0])
    return r.results[0]["out_0"]
```

```python
from contextlib import ExitStack

import concourse.bass as bass
from concourse import mybir

ALU = mybir.AluOpType
ACT = mybir.ActivationFunctionType
AX = mybir.AxisListType
F32 = mybir.dt.float32
I32 = mybir.dt.int32
BF16 = mybir.dt.bfloat16

P = 128
EPS = 1e-5
BIG = 3.0e38


def after(eng, sem, value):
    if not isinstance(value, int) or value > 0:
        eng.wait_ge(sem, value)


def run_steps(eng, first, last, steady_from, steady_to, step):
    for i in range(first, steady_from):
        step(i, i)
    pairs = (steady_to - steady_from) // 2
    with eng.Fori(0, pairs) as pair:
        for u in range(2):
            step(pair * 2 + (steady_from + u), steady_from + u)
    for i in range(steady_from + 2 * pairs, last):
        step(i, i)


def xattn_moe_kernel(nc, x, ctx_in, wqg, bqg, wkg, bkg, wvg, bvg, wql, bql, wkl, bkl, wvl, bvl, wp, bp,
                     gate_w, w1, b1, w2, b2, out):
    T, _, D = x.shape
    E, _, F = w1.shape
    C = D // P
    FC = F // P
    NH = 4
    HD = D // NH
    TOKENS = T * P
    NB = 2 * TOKENS // P + E - 1
    ROWS = TOKENS + P
    SCALE = float(D) ** -0.5
    GROUPS = 4
    TG = T // GROUPS

    xn_dram = nc.dram_tensor("xn_rows", (ROWS, D), F32, kind="Internal").ap()
    acc_dram = nc.dram_tensor("acc_rows", (ROWS, D), F32, kind="Internal").ap()
    out_rows = out.rearrange("b s d -> (b s) d")

    with ExitStack() as ctx:
        def sb(name, shape, dt=F32):
            return ctx.enter_context(nc.sbuf_tensor(name, shape, dt))

        def sem(name):
            return ctx.enter_context(nc.semaphore(name))

        W1 = sb("W1", [P, E, C, F])
        W2 = sb("W2", [P, E, FC, D])
        X = sb("X", [P, T, D])
        XW = X[:, :, :].rearrange("p t d -> p (t d)")\
            .rearrange("p (n c f) -> p n c f", n=2, c=C)
        CX = sb("CX", [P, 2, NH, 2, HD])
        def carver(whole):
            used = [0]

            def piece(*shape):
                n = 1
                for s in shape:
                    n *= s
                a = whole[:, used[0]:used[0] + n]
                used[0] += n
                names = "abcd"[:len(shape)]
                return a.rearrange(f"p ({' '.join(names)}) -> p {' '.join(names)}", **dict(zip(names, shape)))

            return piece

        shared = sb("shared", [P, 30 * D])
        att = carver(shared)
        rout = carver(shared)
        exs = carver(shared)
        QW = att(2, D)
        QB = att(2, D)
        KW = att(2, D)
        KB = att(2, D)
        BP = att(D)
        ident = sb("ident", [P, P])
        ones = sb("ones", [P, P])
        tri = sb("tri", [P, P])
        vrows = sb("vrows", [NH * 2 + C, P])
        vcols = sb("vcols", [P, NH * 2 + C])
        b2rows = sb("b2rows", [E, D])
        b2rest = sb("b2rest", [E, D])
        b2part = sb("b2part", [E, 3, D], BF16)
        b1rows = sb("b1rows", [E * FC, P])
        b1T = sb("b1T", [P, E * FC])
        GW = sb("GW", [P, C, E])
        half = sb("half", [P, 1])
        eps = sb("eps", [P, 1])
        st6 = sb("st6", [P, 2, 6])
        mv = sb("mv", [P, 2, 2, 2])
        rs = sb("rs", [P, 2, 2])
        qu = att(2, D)
        q = att(2, 2, D)
        k = att(2, 2, D)
        nmax = sb("nmax", [P, 2, 4])
        ex = att(2, 4, HD)
        pr = att(2, 4, HD)
        rsum = sb("rsum", [P, 2, 4])
        rinv = sb("rinv", [P, 2, 4])
        rw = sb("rw", [P, 2, 4])
        aT = att(C, P)
        vT = att(2, NH, P)
        xn = sb("xn", [P, 2, D])
        xnT = sb("xnT", [P, C, P])
        L = sb("L", [P, T, E])
        iotaE = sb("iotaE", [P, E])
        iotaB = sb("iotaB", [P, NB])
        iotaR = sb("iotaR", [P, P])
        tokid = sb("tokid", [P, T])
        slotno = sb("slotno", [P, 1])
        segm = sb("segm", [P, E, T])
        m12 = sb("m12", [P, 2, T])
        mask = rout(2, T * E)
        mk = [mask[:, n, :].rearrange("p (t e) -> p t e", e=E) for n in range(2)]
        tmpA = rout(T, E)
        tmpB = rout(T, E)
        tmpC = rout(E, T)
        tmpD = rout(E, T)
        tot = rout(E, T)
        sel = rout(T)
        ew = rout(T)
        den = rout(T)
        wk2 = sb("wk2", [P, 2, T])
        posf = sb("posf", [P, 2, T])
        posi = sb("posi", [P, 2, T], I32)
        slot_i = sb("slot_i", [P, 2, T], I32)
        blk_i = sb("blk_i", [P, 2, T], I32)
        slot_f = sb("slot_f", [P, 2, T])
        blk_f = sb("blk_f", [P, 2, T])
        cnt_i = sb("cnt_i", [P, E], I32)
        cnt_s = sb("cnt_s", [P, E], I32)
        nblk = sb("nblk", [P, E])
        cblk = sb("cblk", [P, E])
        offs = sb("offs", [P, E])
        onesE = sb("onesE", [P, E])
        cmpb = rout(NB, E)
        ebf = sb("ebf", [P, NB])
        expert = sb("expert", [P, NB], I32)
        ohB = rout(2 * T, NB)
        V = rout(2 * T, 2 * NB)
        ohR = rout(16, P)
        tv = sb("tv", [P, NB])
        tw = sb("tw", [P, NB])
        row_of = sb("row_of", [P, NB], I32)
        w_of = sb("w_of", [P, NB])
        gix = sb("gix", [P, 2], I32)
        six = sb("six", [P, 2], I32)
        XG = exs(2, D)
        XT = exs(2, C, P)
        hb = exs(FC, P)
        hT = exs(2, FC, P)
        Y = exs(2, D)
        B2 = sb("B2", [3, E, D], BF16)
        ones3 = sb("ones3", [3, P], BF16)

        ps = [ctx.enter_context(nc.psum_tensor(f"bank{n}", [P, 512], F32)) for n in range(8)]
        pS = [ps[n][:, 0:4 * HD].rearrange("p (c g e) -> p c g e", c=C, g=2) for n in range(2)]
        pCT = [ps[n][:, :].rearrange("p (h n) -> p h n", h=NH) for n in (2, 7)]
        pAT = ps[3][:, 0:D].rearrange("p (c d) -> p c d", c=C)
        pO = ps[4][:, 0:D]
        pXT = ps[5][:, 0:D].rearrange("p (c n) -> p c n", c=C)
        pL = ps[6][:, 0:T * E].rearrange("p (t e) -> p t e", e=E)
        pMisc = ps[6][:, T * E:3 * T * E]
        pTok = ps[7][:, 0:2 * NB]
        pHT = [[ps[2 * n + m][:, :].rearrange("p (c n) -> p c n", n=P) for m in range(2)] for n in range(2)]
        pY = [ps[4][:, 0:D], ps[5][:, 0:D]]
        pGT = ps[6][:, 0:D].rearrange("p (c n) -> p c n", c=C)

        x_in = [sem(f"x_in{g}") for g in range(GROUPS)]
        c_in = [sem(f"c_in{n}") for n in range(2)]
        kc_in, qc_in, bp_in, v_in, w_in = sem("kc_in"), sem("qc_in"), sem("bp_in"), sem("v_in"), sem("w_in")
        b2_in, b2_cut, b2_placed = sem("b2_in"), sem("b2_cut"), sem("b2_placed")
        w1s_in = [sem(f"w1s_in{n}") for n in range(2)]
        zero_out = sem("zero_out")
        xn_out = [sem(f"xn_out{n}") for n in range(2)]
        x1_out = sem("x1_out")
        acc_in = [sem(f"acc_in{g}") for g in range(2 * GROUPS)]
        res_out = sem("res_out")
        made = sem("made")
        zeroed = sem("zeroed")
        kscaled = sem("kscaled")
        vtr, vcopied = sem("vtr"), sem("vcopied")
        st1a, st1, rsa, rs_ok = sem("st1a"), sem("st1"), sem("rsa"), sem("rs_ok")
        qmul, q_ok, kmul, k_ok, xb_ok = sem("qmul"), sem("q_ok"), sem("kmul"), sem("k_ok"), sem("xb_ok")
        s_ok, max_ok, exp_ok, inv_ok, rw_ok, pr_ok = (sem("s_ok"), sem("max_ok"), sem("exp_ok"), sem("inv_ok"),
                                                      sem("rw_ok"), sem("pr_ok"))
        ct_ok, vt_ok, at_ok, as_ok, o_ok = sem("ct_ok"), sem("vt_ok"), sem("at_ok"), sem("as_ok"), sem("o_ok")
        x1_ok, st2a, st2, xn_ok = sem("x1_ok"), sem("st2a"), sem("st2"), sem("xn_ok")
        xt_ok, xts_ok, l_ok = sem("xt_ok"), sem("xts_ok"), sem("l_ok")
        waited_pool, waited_dve = sem("waited_pool"), sem("waited_dve")
        route = sem("route")
        gap_ok, gate_exp = sem("gap_ok"), sem("gate_exp")
        mask_ok, rank_ok = sem("mask_ok"), sem("rank_ok")
        ohr_ok, table_mm, tok_ok = sem("ohr_ok"), sem("table_mm"), sem("tok_ok")
        gix_ok, six_ok = sem("gix_ok"), sem("six_ok")
        xg_ok = [sem(f"xg_ok{n}") for n in range(2)]
        gt_ok, gts_ok, h_ok, hb_ok, gelu_ok, y_ok, ys_ok, added = (
            sem("gt_ok"), sem("gts_ok"), sem("h_ok"), sem("hb_ok"), sem("gelu_ok"), sem("y_ok"), sem("ys_ok"),
            sem("added"))

        MADE = 13
        RS_FIRST = -3
        A_FIRST, A_LAST = -4, T + 4
        A_FROM, A_TO = 4, T - 4
        B_LAST = NB + 2
        B_FROM, B_TO = 3, NB - 2
        B_TO -= (B_TO - B_FROM) % 2
        assert (A_TO - A_FROM) % 2 == 0

        def tile_on(i):
            return not isinstance(i, int) or 0 <= i < T

        def block_on(i):
            return not isinstance(i, int) or 0 <= i < NB

        def group_loaded(eng, sems, t):
            if isinstance(t, int):
                eng.wait_ge(sems[t // TG], 16)
            else:
                for s in sems:
                    eng.wait_ge(s, 16)

        block = ctx.enter_context(nc.Block())

        @block.sync
        def _(sp):
            def row(a):
                return a.partition_broadcast(P)

            def load_group(dst, src, g, s):
                sp.dma_start(dst[:, g * TG:(g + 1) * TG, :],
                             src[g * TG:(g + 1) * TG].rearrange("t p d -> p t d")).then_inc(s, 16)

            load_group(X, x, 0, x_in[0])

            def load_ctx(t, n):
                for r in range(2):
                    sp.dma_start(CX[:, n, :, r, :], ctx_in[bass.ds(t, 1)].rearrange("a p (h e) -> p (a h) e", e=HD))\
                      .then_inc(c_in[n], 16)

            load_ctx(0, 0)
            for dst, srcs in ((KW, (wkg, wkl)), (KB, (bkg, bkl))):
                for n, src in enumerate(srcs):
                    sp.dma_start(dst[:, n, :], row(src)).then_inc(kc_in, 16)
            for dst, srcs in ((QW, (wqg, wql)), (QB, (bqg, bql))):
                for n, src in enumerate(srcs):
                    sp.dma_start(dst[:, n, :], row(src)).then_inc(qc_in, 16)
            load_ctx(1, 1)
            load_group(X, x, 1, x_in[1])
            sp.dma_start(BP[:, :], row(bp)).then_inc(bp_in, 16)
            for g in range(2, GROUPS):
                load_group(X, x, g, x_in[g])
            sp.wait_ge(zeroed, 1)
            sp.dma_start(xn_dram[TOKENS:ROWS, :], pr[:, 0].rearrange("p a d -> p (a d)")).then_inc(zero_out, 16)
            sp.dma_start(acc_dram[TOKENS:ROWS, :], pr[:, 0].rearrange("p a d -> p (a d)")).then_inc(zero_out, 16)

            def tiles(i, u):
                t = i + 4
                if tile_on(t) and not (isinstance(t, int) and t < 2):
                    sp.wait_ge(k_ok, t - 1)
                    sp.wait_ge(ct_ok, t - 1)
                    load_ctx(t, u % 2)
                t = i - 1
                if tile_on(t):
                    sp.wait_ge(x1_ok, t + 1)
                    sp.dma_start(acc_dram[bass.ds(t * P, P), :], X[:, bass.ds(t, 1), :].rearrange("p a d -> p (a d)"))\
                      .then_inc(x1_out, 16)
                t, n = i - 2, u % 2
                if tile_on(t):
                    sp.wait_ge(xn_ok, t + 1)
                    sp.dma_start(xn_dram[bass.ds(t * P, P), :], xn[:, n, :]).then_inc(xn_out[n], 16)
                j = i
                if tile_on(j):
                    sp.dma_start(W1[:, :, :, :].rearrange("p e c f -> p (e c) f")[:, bass.ds(j, 1), :]
                                 .rearrange("p a f -> p (a f)"),
                                 w1.rearrange("e (c p) f -> (e c) p f", p=P)[bass.ds(j, 1)]
                                 .rearrange("a p f -> p (a f)")).then_inc(w_in, 16)
                    sp.dma_start(W2[:, :, :, :].rearrange("p e (h c) d -> p (e h) c d", h=2)[:, bass.ds(j, 1)]
                                 .rearrange("p a c d -> p (a c) d"),
                                 w2.rearrange("e (h c p) d -> (e h) p c d", h=2, p=P)[bass.ds(j, 1)]
                                 .rearrange("a p c d -> p (a c) d")).then_inc(w_in, 16)

            run_steps(sp, -2, T + 2, A_FROM, A_TO, tiles)

            sp.wait_ge(tok_ok, 3)
            sp.wait_ge(x1_out, 16 * T)
            sp.wait_ge(w_in, 16 * 2 * T)

            def stage(b, n):
                if block_on(b):
                    e = sp.value_load(expert[0:1, bass.ds(b, 1)], min_val=0, max_val=E - 1)
                    after(sp, h_ok, 2 * (b - 1))
                    sp.dma_start(XW[:, n], W1[:, bass.ds(e, 1)].rearrange("p a c f -> p (a c) f"))\
                      .then_inc(w1s_in[n], 16)

            run_steps(sp, 0, NB, B_FROM, B_TO, lambda i, u: stage(i, u % 2))

            TH = TG // 2
            sp.wait_ge(added, 16 * NB)
            for g in range(2 * GROUPS):
                rows = slice(g * TH * P, (g + 1) * TH * P)
                sp.dma_start(X[:, g * TH:(g + 1) * TH, :], acc_dram[rows, :].rearrange("(t p) d -> p t d", p=P))\
                  .then_inc(acc_in[g], 16)
            sp.wait_ge(res_out, 16 * 2 * GROUPS)

        @block.gpsimd
        def _(pool):
            pool.memset(pr[:, 0], 0.0).then_inc(zeroed, 1)
            pool.memset(half[:, :], -0.5).then_inc(made, 1)
            pool.memset(eps[:, :], EPS).then_inc(made, 1)
            pool.memset(ident[:, :], 0.0).then_inc(made, 1)
            pool.memset(ones[:, :], 1.0).then_inc(made, 1)
            pool.wait_ge(made, 4)
            pool.affine_select(out=ident[:, :], in_=ident[:, :], compare_op=ALU.not_equal, fill=1.0, base=0,
                               pattern=[[-1, P]], channel_multiplier=1).then_inc(made, 1)
            pool.affine_select(out=tri[:, :], in_=ones[:, :], compare_op=ALU.is_ge, fill=0.0, base=-1,
                               pattern=[[1, P]], channel_multiplier=-1).then_inc(made, 1)
            pool.iota(iotaE[:, :], pattern=[[1, E]], base=-E, channel_multiplier=0,
                      allow_small_or_imprecise_dtypes=True).then_inc(made, 1)
            pool.iota(iotaB[:, :], pattern=[[1, NB]], base=0, channel_multiplier=0,
                      allow_small_or_imprecise_dtypes=True).then_inc(made, 1)
            pool.iota(iotaR[:, :], pattern=[[1, P]], base=0, channel_multiplier=0,
                      allow_small_or_imprecise_dtypes=True).then_inc(made, 1)
            pool.iota(tokid[:, :], pattern=[[P, T]], base=-TOKENS, channel_multiplier=1,
                      allow_small_or_imprecise_dtypes=True).then_inc(made, 1)
            pool.iota(slotno[:, :], pattern=[[0, 1]], base=0, channel_multiplier=1,
                      allow_small_or_imprecise_dtypes=True).then_inc(made, 1)
            pool.memset(onesE[:, :], 1.0).then_inc(made, 1)
            pool.memset(ones3[:, :], 1.0).then_inc(made, 1)
            pool.memset(segm[:, :, :], 1.0).then_inc(zeroed, 1)
            pool.wait_ge(zeroed, 2)
            pool.memset(segm[:, :, 0:1], 0.0).then_inc(zeroed, 1)

            def attention(i, u):
                t, t2, r = i + 3, i - 2, (u + 1) % 2
                if tile_on(t) or tile_on(t2):
                    ln = slice(0 if tile_on(t) else 1, 2 if tile_on(t2) else 1)
                    var, inv = mv[:, r, ln, 1:2], rs[:, r, ln].rearrange("p (l o) -> p l o", o=1)
                    cols = [P, ln.stop - ln.start, 1]
                    if tile_on(t):
                        after(pool, q_ok, t - 1)
                        pool.wait_ge(st1, t + 1)
                    if tile_on(t2):
                        after(pool, xn_ok, t2 - 1)
                        pool.wait_ge(st2, t2 + 1)
                    pool.tensor_tensor(inv, var, eps[:, :].rearrange("p (l o) -> p l o", o=1).broadcast_to(cols), ALU.add)\
                        .then_inc(rsa, 1)
                    pool.wait_ge(rsa, i + (1 - RS_FIRST))
                    pool.tensor_tensor(inv, inv, half[:, :].rearrange("p (l o) -> p l o", o=1).broadcast_to(cols), ALU.pow)\
                        .then_inc(rs_ok, 1)
                t, n = i + 2, u % 2
                if tile_on(t):
                    pool.wait_ge(c_in[n], 16 * (t - n) + 32)
                    pool.wait_ge(kscaled, 2)
                    after(pool, s_ok, t - 1)
                    c = CX[:, n].rearrange("p h g e -> p g h e")
                    pool.tensor_tensor(k[:, n].rearrange("p g (h e) -> p g h e", e=HD), c,
                                       KW.rearrange("p g (h e) -> p g h e", e=HD), ALU.mult).then_inc(kmul, 1)
                    pool.wait_ge(kmul, t + 1)
                    pool.tensor_tensor(k[:, n], k[:, n], KB[:, :, :], ALU.add).then_inc(k_ok, 1)
                t = i
                if tile_on(t):
                    xt = X[:, bass.ds(t, 1), :].rearrange("p a d -> p (a d)")
                    pool.wait_ge(q_ok, t + 1)
                    pool.wait_ge(bp_in, 16)
                    pool.tensor_tensor(xt, xt, BP[:, :], ALU.add).then_inc(xb_ok, 1)

            run_steps(pool, A_FIRST, A_LAST, A_FROM, A_TO, attention)

            pool.wait_ge(tok_ok, 2)
            pool.wait_ge(zero_out, 32)
            pool.wait_ge(xn_out[0], 16 * (T // 2))

            def experts(i, u):
                b, n = i + 2, u % 2
                if block_on(b):
                    after(pool, xg_ok[n], 8 * (b - n))
                    pool.tensor_copy(gix[:, n:n + 1], row_of[:, bass.ds(b, 1)]).then_inc(gix_ok, 1)
                    pool.wait_ge(xn_out[1], 16 * (T // 2))
                    pool.wait_ge(gix_ok, b + 1)
                    after(pool, gt_ok, b - 1)
                    pool.sem_inc(waited_pool, 1)
                    pool.indirect_dma_start(out=XG[:, n, :], out_offset=None, in_=xn_dram,
                                            in_offset=bass.IndirectOffsetOnAxis(ap=gix[:, n:n + 1], axis=0))\
                        .then_inc(xg_ok[n], 16)
                b, n = i - 2, u % 2
                if block_on(b):
                    after(pool, added, 16 * b)
                    pool.tensor_copy(six[:, n:n + 1], row_of[:, bass.ds(b, 1)]).then_inc(six_ok, 1)
                    pool.wait_ge(x1_out, 16 * T)
                    pool.wait_ge(six_ok, b + 1)
                    pool.wait_ge(ys_ok, b + 1)
                    pool.sem_inc(waited_pool, 1)
                    pool.indirect_dma_start(out=acc_dram,
                                            out_offset=bass.IndirectOffsetOnAxis(ap=six[:, n:n + 1], axis=0),
                                            in_=Y[:, n, :], in_offset=None, compute_op=ALU.add,
                                            bounds_check=ROWS - 1, oob_is_err=True).then_inc(added, 16)

            run_steps(pool, -2, B_LAST, B_FROM, B_TO, experts)

        @block.scalar
        def _(act):
            for r, (wv, bv) in enumerate(((wvg, bvg), (wvl, bvl))):
                for m, src in enumerate((wv, bv)):
                    act.dma_start(vrows[m * NH:(m + 1) * NH, r * HD:(r + 1) * HD], src.rearrange("(h e) -> h e", e=HD))\
                       .then_inc(v_in, 16)
            act.dma_start(vrows[2 * NH:2 * NH + C, :], wp.rearrange("(c p) -> c p", p=P)).then_inc(v_in, 16)
            act.dma_start(b1rows[:, :], b1.rearrange("e (c p) -> (e c) p", p=P)).then_inc(v_in, 16)
            act.dma_start(GW[:, :, :], gate_w.rearrange("(c p) e -> p c e", p=P)).then_inc(v_in, 16)
            act.dma_start(b2rows[:, :], b2).then_inc(b2_in, 16)
            act.wait_ge(kc_in, 16 * 4)
            act.activation(KW[:, :, :], KW[:, :, :], ACT.Copy, scale=SCALE).then_inc(kscaled, 1)
            act.activation(KB[:, :, :], KB[:, :, :], ACT.Copy, scale=SCALE).then_inc(kscaled, 1)
            act.wait_ge(vtr, 2)
            act.activation(vcols[:, :], pMisc[:, 0:2 * NH + C], ACT.Copy).then_inc(vcopied, 1)
            act.activation(b1T[:, :], pMisc[:, 64:64 + E * FC], ACT.Copy).then_inc(vcopied, 1)
            act.wait_ge(vcopied, 2)
            act.activation(vcols[:, 2 * NH:], vcols[:, 2 * NH:], ACT.Copy, scale=2.0).then_inc(vcopied, 1)

            def attention(i, u):
                t = i - 1
                if tile_on(t):
                    act.wait_ge(at_ok, t + 1)
                    after(act, o_ok, t)
                    act.activation(aT, pAT, ACT.Copy).then_inc(as_ok, 1)
                t, n = i, u % 2
                if tile_on(t):
                    act.wait_ge(max_ok, t + 1)
                    after(act, pr_ok, t - 1)
                    for a in range(4):
                        act.activation(ex[:, n, a, :], pS[n][:, a // 2, a % 2, :], ACT.Exp, bias=nmax[:, n, a:a + 1],
                                       accum_out=rsum[:, n, a:a + 1]).then_inc(exp_ok, 1)
                t, n = i + 1, (u + 1) % 2
                if tile_on(t):
                    act.wait_ge(ct_ok, t + 1)
                    after(act, o_ok, t - 1)
                    for h in range(NH):
                        act.activation(vT[:, n, h, :], pCT[n][:, h, :], ACT.Identity,
                                       bias=vcols[:, NH + h:NH + h + 1], scale=vcols[:, h:h + 1]).then_inc(vt_ok, 1)

            run_steps(act, A_FIRST, A_LAST, A_FROM, A_TO, attention)

            act.wait_ge(b2_cut, 5)
            for r in range(3):
                act.dma_start(B2[r:r + 1, :, :], b2part[:, r, :]).then_inc(b2_placed, 16)
            act.wait_ge(gap_ok, 1)
            act.activation(ew, sel, ACT.Exp).then_inc(gate_exp, 1)

            def experts(i, u):
                b, n = i, u % 2
                if block_on(b):
                    after(act, y_ok, b - 1)
                    for m in range(2):
                        act.wait_ge(hb_ok, 2 * b + (m + 1))
                        act.activation(hT[:, n, 4 * m:4 * m + 4, :], hb[:, 4 * m:4 * m + 4, :], ACT.Gelu)\
                           .then_inc(gelu_ok, 1)

            run_steps(act, 0, B_LAST, B_FROM, B_TO, experts)

            TH = TG // 2
            for g in range(2 * GROUPS):
                rows = slice(g * TH * P, (g + 1) * TH * P)
                act.wait_ge(acc_in[g], 16)
                act.dma_start(out_rows[rows, :].rearrange("(t p) d -> p t d", p=P), X[:, g * TH:(g + 1) * TH, :])\
                   .then_inc(res_out, 16)

        @block.vector
        def _(dve):
            dve.wait_ge(b2_in, 16)
            cuts = [0]

            def cut(ins):
                ins.then_inc(b2_cut, 1)
                cuts[0] += 1
                dve.wait_ge(b2_cut, cuts[0])

            cut(dve.tensor_copy(b2part[:, 0, :], b2rows[:, :]))
            cut(dve.tensor_tensor(b2rest[:, :], b2rows[:, :], b2part[:, 0, :], ALU.subtract))
            cut(dve.tensor_copy(b2part[:, 1, :], b2rest[:, :]))
            cut(dve.tensor_tensor(b2rest[:, :], b2rest[:, :], b2part[:, 1, :], ALU.subtract))
            cut(dve.tensor_copy(b2part[:, 2, :], b2rest[:, :]))

            def attention(i, u):
                t, n = i, u % 2
                if tile_on(t):
                    dve.wait_ge(s_ok, t + 1)
                    after(dve, exp_ok, 4 * (t - 1))
                    dve.tensor_reduce(nmax[:, n, :], pS[n].rearrange("p c g e -> p (c g) e"), AX.X, ALU.max,
                                      negate=True).then_inc(max_ok, 1)
                t, n = i + 2, u % 2
                if tile_on(t):
                    xb = X[:, bass.ds(t, 1), :].broadcast_to([P, 2, D])
                    dve.wait_ge(rs_ok, t + 1)
                    dve.wait_ge(qc_in, 16 * 4)
                    after(dve, q_ok, t)
                    dve.scalar_tensor_tensor(out=qu, in0=xb, scalar=mv[:, n, 0, 0:1], in1=QW,
                                             op0=ALU.subtract, op1=ALU.mult).then_inc(qmul, 1)
                    after(dve, s_ok, t - 1)
                    dve.wait_ge(qmul, t + 1)
                    dve.scalar_tensor_tensor(out=q[:, n], in0=qu, scalar=rs[:, n, 0:1],
                                             in1=QB, op0=ALU.mult, op1=ALU.add).then_inc(q_ok, 1)
                t, n = i + 4, u % 2
                if tile_on(t):
                    group_loaded(dve, x_in, t)
                    after(dve, st1, t)
                    dve.sem_inc(waited_dve, 1)
                    dve.bn_stats(st6[:, 0, :], X[:, bass.ds(t, 1), :].rearrange("p a d -> p (a d)")).then_inc(st1a, 1)
                    dve.wait_ge(st1a, t + 1)
                    after(dve, qmul, t - 1)
                    after(dve, rsa, t - 1)
                    dve.sem_inc(waited_dve, 1)
                    dve.bn_aggr(mv[:, n, 0, :], st6[:, 0, :]).then_inc(st1, 1)
                t, n = i, u % 2
                if tile_on(t):
                    dve.wait_ge(exp_ok, 4 * (t + 1))
                    dve.reciprocal(rinv[:, n, :], rsum[:, n, :]).then_inc(inv_ok, 1)
                    dve.wait_ge(inv_ok, t + 1)
                    dve.wait_ge(vcopied, 3)
                    dve.tensor_tensor(rw[:, n, :].rearrange("p (c g) -> p c g", c=C),
                                      rinv[:, n, :].rearrange("p (c g) -> p c g", c=C),
                                      vcols[:, 2 * NH:].rearrange("p (c o) -> p c o", o=1).broadcast_to([P, C, 2]),
                                      ALU.mult).then_inc(rw_ok, 1)
                    dve.wait_ge(rw_ok, t + 1)
                    after(dve, at_ok, t - 1)
                    dve.wait_ge(zero_out, 32)
                    dve.tensor_tensor(pr[:, n], ex[:, n],
                                      rw[:, n, :].rearrange("p (a b) -> p a b", b=1).broadcast_to([P, 4, HD]),
                                      ALU.mult).then_inc(pr_ok, 1)
                t, n = i - 1, u % 2
                if tile_on(t):
                    xt = X[:, bass.ds(t, 1), :].rearrange("p a d -> p (a d)")
                    dve.wait_ge(xb_ok, t + 1)
                    dve.wait_ge(o_ok, t + 1)
                    dve.tensor_tensor(xt, pO, xt, ALU.add).then_inc(x1_ok, 1)
                    dve.wait_ge(x1_ok, t + 1)
                    after(dve, st2, t)
                    dve.sem_inc(waited_dve, 1)
                    dve.bn_stats(st6[:, 1, :], xt).then_inc(st2a, 1)
                    dve.wait_ge(st2a, t + 1)
                    after(dve, xn_ok, t - 1)
                    after(dve, rsa, t + (1 - RS_FIRST))
                    dve.sem_inc(waited_dve, 1)
                    dve.bn_aggr(mv[:, n, 1, :], st6[:, 1, :]).then_inc(st2, 1)
                t, n = i - 2, u % 2
                if tile_on(t):
                    dve.wait_ge(rs_ok, t + (3 - RS_FIRST))
                    after(dve, xn_out[n], 8 * (t - n))
                    after(dve, xt_ok, t - 1)
                    dve.tensor_scalar(xn[:, n, :], X[:, bass.ds(t, 1), :].rearrange("p a d -> p (a d)"),
                                      mv[:, (u + 1) % 2, 1, 0:1], rs[:, (u + 1) % 2, 1:2], ALU.subtract, ALU.mult)\
                       .then_inc(xn_ok, 1)
                t = i - 3
                if tile_on(t):
                    dve.wait_ge(xt_ok, t + 1)
                    after(dve, l_ok, t)
                    dve.tensor_copy(xnT[:, :, :], pXT).then_inc(xts_ok, 1)

            run_steps(dve, A_FIRST, A_LAST, A_FROM, A_TO, attention)

            steps = [0]

            def chain(ins):
                ins.then_inc(route, 1)
                steps[0] += 1
                dve.wait_ge(route, steps[0])

            def over_e(a):
                return a.rearrange("p (t o) -> p t o", o=1).broadcast_to([P, T, E])

            iota_te = iotaE[:, :].rearrange("p (o e) -> p o e", o=1).broadcast_to([P, T, E])
            dve.wait_ge(zeroed, 3)
            dve.wait_ge(l_ok, T)
            dve.wait_ge(made, MADE)
            chain(dve.tensor_copy(L[:, :, :], pL))
            logits = L[:, :, :]
            for n in range(2):
                best = m12[:, n, :]
                chain(dve.tensor_reduce(best, logits, AX.X, ALU.max))
                chain(dve.tensor_tensor(tmpA, logits, over_e(best), ALU.is_equal))
                chain(dve.tensor_tensor(tmpA, tmpA, iota_te, ALU.mult))
                chain(dve.tensor_reduce(sel, tmpA, AX.X, ALU.min))
                chain(dve.tensor_tensor(mk[n], iota_te, over_e(sel), ALU.is_equal))
                if n == 0:
                    chain(dve.scalar_tensor_tensor(out=tmpB, in0=mk[0], scalar=-BIG, in1=logits,
                                                   op0=ALU.mult, op1=ALU.add))
                    logits = tmpB
            dve.tensor_tensor(tmpA, mk[0], mk[1], ALU.add).then_inc(mask_ok, 1)
            dve.tensor_tensor(sel, m12[:, 1, :], m12[:, 0, :], ALU.subtract).then_inc(gap_ok, 1)
            dve.wait_ge(gate_exp, 1)
            chain(dve.tensor_scalar(den, ew, 1.0, None, ALU.add))
            chain(dve.reciprocal(wk2[:, 0, :], den))
            chain(dve.tensor_tensor(wk2[:, 1, :], ew, wk2[:, 0, :], ALU.mult))
            dve.wait_ge(rank_ok, 1)
            pR = pMisc[:, 0:T * E].rearrange("p (t e) -> p t e", e=E)
            pTot = pMisc[:, T * E:2 * T * E].rearrange("p (t e) -> p e t", e=E)
            chain(dve.tensor_copy(tot, pTot))
            chain(dve.tensor_tensor_scan(tmpC.rearrange("p e t -> p (e t)"), segm[:, :, :].rearrange("p e t -> p (e t)"),
                                         tot.rearrange("p e t -> p (e t)"), 0.0, ALU.mult, ALU.add))
            last = tmpC[:, :, T - 1:T].rearrange("p e o -> p (e o)")
            chain(dve.tensor_scalar(cnt_i[:, :], last, float(P - 1), None, ALU.add))
            chain(dve.tensor_scalar(cnt_s[:, :], cnt_i[:, :], 7, None, ALU.arith_shift_right))
            chain(dve.tensor_copy(nblk[:, :], cnt_s[:, :]))
            chain(dve.tensor_tensor_scan(cblk[:, :], onesE[:, :], nblk[:, :], 0.0, ALU.mult, ALU.add))
            chain(dve.tensor_tensor(offs[:, :], cblk[:, :], nblk[:, :], ALU.subtract))
            chain(dve.tensor_scalar(offs[:, :], offs[:, :], float(P), None, ALU.mult))
            chain(dve.tensor_tensor(tmpD, tmpC, tot, ALU.subtract))
            chain(dve.tensor_tensor(tmpD, tmpD, offs[:, :].rearrange("p (e o) -> p e o", o=1).broadcast_to([P, E, T]),
                                    ALU.add))
            chain(dve.tensor_tensor(tmpA, pR, tmpD.rearrange("p e t -> p t e"), ALU.add))
            for n in range(2):
                chain(dve.tensor_tensor(tmpB, tmpA, mk[n], ALU.mult))
                chain(dve.tensor_reduce(posf[:, n, :], tmpB, AX.X, ALU.add))
            chain(dve.tensor_copy(posi[:, :, :], posf[:, :, :]))
            chain(dve.tensor_scalar(slot_i[:, :, :], posi[:, :, :], P - 1, None, ALU.bitwise_and))
            chain(dve.tensor_scalar(blk_i[:, :, :], posi[:, :, :], 7, None, ALU.arith_shift_right))
            chain(dve.tensor_copy(slot_f[:, :, :], slot_i[:, :, :]))
            chain(dve.tensor_copy(blk_f[:, :, :], blk_i[:, :, :]))
            N2 = 2 * T

            def flat(a):
                return a.rearrange("p n (t o) -> p (n t) o", o=1).broadcast_to([P, N2, NB])

            chain(dve.tensor_tensor(ohB, iotaB[:, :].rearrange("p (o b) -> p o b", o=1).broadcast_to([P, N2, NB]),
                                    flat(blk_f[:, :, :]), ALU.is_equal))
            for n in range(2):
                dve.tensor_tensor(V[:, n * T:(n + 1) * T, 0:NB], ohB[:, n * T:(n + 1) * T, :],
                                  tokid[:, :].rearrange("p (t o) -> p t o", o=1).broadcast_to([P, T, NB]), ALU.mult)
            chain(dve.tensor_tensor(V[:, :, NB:2 * NB], ohB, flat(wk2[:, :, :]), ALU.mult))

            slots = slot_f[:, :, :].rearrange("p n (t o) -> p (n t) o", o=1)
            for h in range(N2 // 4):
                r = h % 4
                after(dve, table_mm, 4 * (h - 3))
                dve.tensor_tensor(ohR[:, 4 * r:4 * r + 4, :],
                                  iotaR[:, :].rearrange("p (o s) -> p o s", o=1).broadcast_to([P, 4, P]),
                                  slots[:, 4 * h:4 * h + 4].broadcast_to([P, 4, P]), ALU.is_equal).then_inc(ohr_ok, 1)
            chain(dve.tensor_tensor(cmpb, iotaB[:, :].rearrange("p (b o) -> p b o", o=1).broadcast_to([P, NB, E]),
                                    cblk[:, :].rearrange("p (o e) -> p o e", o=1).broadcast_to([P, NB, E]), ALU.is_ge))
            chain(dve.tensor_reduce(ebf[:, :], cmpb, AX.X, ALU.add))
            dve.tensor_scalar(expert[:, :], ebf[:, :], float(E - 1), None, ALU.min).then_inc(tok_ok, 1)
            dve.wait_ge(table_mm, N2)
            chain(dve.tensor_scalar(tv[:, :], pTok[:, 0:NB], 0.0, None, ALU.is_ge))
            chain(dve.tensor_scalar(tw[:, :], pTok[:, 0:NB], float(TOKENS), None, ALU.add))
            chain(dve.tensor_scalar(tv[:, :], tv[:, :], slotno[:, 0:1], None, ALU.mult))
            dve.tensor_tensor(row_of[:, :], tw[:, :], tv[:, :], ALU.add).then_inc(tok_ok, 1)
            dve.tensor_copy(w_of[:, :], pTok[:, NB:2 * NB]).then_inc(tok_ok, 1)
            dve.wait_ge(tok_ok, 3)

            def experts(i, u):
                b, n = i + 1, (u + 1) % 2
                if block_on(b):
                    dve.wait_ge(gt_ok, b + 1)
                    after(dve, h_ok, 2 * (b - 1))
                    dve.tensor_copy(XT[:, n], pGT).then_inc(gts_ok, 1)
                b, n = i, u % 2
                if block_on(b):
                    e = dve.value_load(expert[0:1, bass.ds(b, 1)], min_val=0, max_val=E - 1)
                    for m in range(2):
                        dve.wait_ge(h_ok, 2 * b + (m + 1))
                        after(dve, gelu_ok, 2 * b + (m - 1) if not isinstance(b, int) else 2 * b + m - 1)
                        dve.tensor_tensor(hb[:, 4 * m:4 * m + 4, :], pHT[n][m],
                                          b1T[:, bass.ds(e * FC + 4 * m, 4)].rearrange("p (c o) -> p c o", o=1)
                                          .broadcast_to([P, 4, P]), ALU.add).then_inc(hb_ok, 1)
                b, n = i - 1, (u - 1) % 2
                if block_on(b):
                    dve.wait_ge(y_ok, b + 1)
                    after(dve, added, 16 * (b - 1))
                    dve.tensor_scalar(Y[:, n, :], pY[n], w_of[:, bass.ds(b, 1)], None, ALU.mult).then_inc(ys_ok, 1)

            run_steps(dve, -1, B_LAST, B_FROM, B_TO, experts)

        @block.tensor
        def _(pe):
            pe.wait_ge(made, MADE)
            pe.wait_ge(v_in, 16 * 7)
            pe.transpose(pMisc[:, 0:2 * NH + C], vrows[:, :], ident[0:2 * NH + C, 0:2 * NH + C]).then_inc(vtr, 1)
            pe.transpose(pMisc[:, 64:64 + E * FC], b1rows[:, :], ident[0:E * FC, 0:E * FC]).then_inc(vtr, 1)

            def attention(i, u):
                t, n = i + 1, (u + 1) % 2
                if tile_on(t):
                    pe.wait_ge(q_ok, t + 1)
                    pe.wait_ge(k_ok, t + 1)
                    after(pe, exp_ok, 4 * (t - 1))
                    for c in range(C):
                        for g in range(2):
                            for h in range(2):
                                ch = slice(c * P + h * HD, c * P + (h + 1) * HD)
                                mm = pe.matmul(pS[n][h * HD:(h + 1) * HD, c, g, :], q[:, n, g, ch], k[:, n, g, ch],
                                               start=True, stop=True)
                    mm.then_inc(s_ok, 1)
                t, n = i + 2, u % 2
                if tile_on(t):
                    pe.wait_ge(c_in[n], 16 * (t - n) + 32)
                    after(pe, vt_ok, 4 * (t - 1))
                    for h in range(NH):
                        mm = pe.transpose(pCT[n][:, h, :],
                                          CX[:, n, h].rearrange("p g e -> p (g e)"), ident[:, :])
                    mm.then_inc(ct_ok, 1)
                t, n = i - 1, (u - 1) % 2
                if tile_on(t):
                    pe.wait_ge(as_ok, t + 1)
                    pe.wait_ge(vt_ok, 4 * (t + 1))
                    after(pe, x1_ok, t)
                    for h in range(NH):
                        mm = pe.matmul(pO[:, h * HD:(h + 1) * HD], vT[:, n, h, :],
                                       aT[:, h // 2, (h % 2) * HD:(h % 2 + 1) * HD], start=True, stop=True)
                    mm.then_inc(o_ok, 1)
                t, n = i - 3, (u - 3) % 2
                if tile_on(t):
                    pe.wait_ge(xn_ok, t + 1)
                    after(pe, xts_ok, t)
                    for c in range(C):
                        mm = pe.transpose(pXT[:, c, :], xn[:, n, c * P:(c + 1) * P], ident[:, :])
                    mm.then_inc(xt_ok, 1)
                t = i - 4
                if tile_on(t):
                    pe.wait_ge(xts_ok, t + 1)
                    for c in range(C):
                        mm = pe.matmul(pL[:, bass.ds(t, 1), :].rearrange("p a e -> p (a e)"), xnT[:, c, :], GW[:, c, :],
                                       start=(c == 0), stop=(c == C - 1))
                    mm.then_inc(l_ok, 1)
                t, n = i, u % 2
                if tile_on(t):
                    pe.wait_ge(pr_ok, t + 1)
                    after(pe, as_ok, t)
                    for c in range(C):
                        mm = pe.transpose(pAT[:, c, :], pr[:, n, 2 * c:2 * c + 2, :].rearrange("p g e -> p (g e)"),
                                          ident[:, :])
                    mm.then_inc(at_ok, 1)

            run_steps(pe, A_FIRST, A_LAST, A_FROM, A_TO, attention)

            pe.wait_ge(mask_ok, 1)
            chosen = tmpA.rearrange("p t e -> p (t e)")
            pe.matmul(pMisc[:, 0:T * E], tri[:, :], chosen, start=True, stop=True)
            pe.matmul(pMisc[:, T * E:2 * T * E], ones[:, :], chosen, start=True, stop=True).then_inc(rank_ok, 1)

            for t in range(2 * T):
                pe.wait_ge(ohr_ok, t // 4 + 1)
                pe.matmul(pTok, ohR[:, t % 16, :], V[:, t, :], start=(t == 0), stop=(t == 2 * T - 1))\
                  .then_inc(table_mm, 1)

            pe.wait_ge(w_in, 16 * 2 * T)
            pe.wait_ge(b2_placed, 16 * 3)
            pe.wait_ge(tok_ok, 3)

            def experts(i, u):
                b, n = i + 1, (u + 1) % 2
                if block_on(b):
                    pe.wait_ge(xg_ok[n], 8 * (b + 2 - n))
                    after(pe, gts_ok, b)
                    for c in range(C):
                        mm = pe.transpose(pGT[:, c, :], XG[:, n, c * P:(c + 1) * P], ident[:, :])
                    mm.then_inc(gt_ok, 1)
                b, n = i, u % 2
                if block_on(b):
                    pe.wait_ge(w1s_in[n], 8 * (b + 2 - n))
                    pe.wait_ge(gts_ok, b + 1)
                    after(pe, hb_ok, 2 * (b - 1))
                    for m in range(2):
                        for f in range(4 * m, 4 * m + 4):
                            for c in range(C):
                                mm = pe.matmul(pHT[n][m][:, f % 4, :], XW[:, n, c, f * P:(f + 1) * P], XT[:, n, c, :],
                                               start=(c == 0), stop=(c == C - 1))
                        mm.then_inc(h_ok, 1)
                b, n = i - 1, (u - 1) % 2
                if block_on(b):
                    e = pe.value_load(expert[0:1, bass.ds(b, 1)], min_val=0, max_val=E - 1)
                    pe.wait_ge(gelu_ok, 2 * (b + 1))
                    after(pe, ys_ok, b - 1)
                    for f in range(FC):
                        pe.matmul(pY[n], hT[:, n, f, :], W2[:, bass.ds(e, 1), f, :].rearrange("p a d -> p (a d)"),
                                  start=(f == 0), stop=False)
                    pe.matmul(pY[n], ones3[:, :], B2[:, bass.ds(e, 1), :].rearrange("p a d -> p (a d)"),
                              start=False, stop=True).then_inc(y_ok, 1)

            run_steps(pe, -1, B_LAST, B_FROM, B_TO, experts)


_INS = ["x", "ctx_1024", "L0_xattn_wqg", "L0_xattn_bqg", "L0_xattn_wkg", "L0_xattn_bkg", "L0_xattn_wvg", "L0_xattn_bvg",
        "L0_xattn_wql", "L0_xattn_bql", "L0_xattn_wkl", "L0_xattn_bkl", "L0_xattn_wvl", "L0_xattn_bvl", "L0_xattn_wp",
        "L0_xattn_bp", "L0_ffn_gate_w", "L0_ffn_w1", "L0_ffn_b1", "L0_ffn_w2", "L0_ffn_b2"]


def kernel(**inputs):
    import numpy as _np
    import concourse.bacc as _bacc
    from concourse import mybir as _mybir
    from concourse.bass_utils import run_bass_kernel_spmd as _run

    nc = _bacc.Bacc("TRN2", target_bir_lowering=False, num_devices=1)
    arrays, args = {}, []
    for name in _INS:
        a = _np.ascontiguousarray(inputs[name])
        arrays[f"in_{name}"] = a
        args.append(nc.dram_tensor(f"in_{name}", a.shape, _mybir.dt.from_np(a.dtype), kind="ExternalInput").ap())
    args.append(nc.dram_tensor("out_0", inputs["x"].shape, _mybir.dt.float32, kind="ExternalOutput").ap())
    xattn_moe_kernel(nc, *args)
    r = _run(nc, [arrays], core_ids=[0])
    return r.results[0]["out_0"]
```

```python
from contextlib import ExitStack

import concourse.bass as bass
from concourse import mybir

ALU = mybir.AluOpType
ACT = mybir.ActivationFunctionType
AX = mybir.AxisListType
F32 = mybir.dt.float32
I32 = mybir.dt.int32
BF16 = mybir.dt.bfloat16
F16 = mybir.dt.float16

P = 128
EPS = 1e-5
BIG = 3.0e38


def after(eng, sem, value):
    if not isinstance(value, int) or value > 0:
        eng.wait_ge(sem, value)


def run_steps(eng, first, last, steady, step):
    begin, end = steady
    for i in range(first, begin):
        step(i, i)
    with eng.Fori(0, (end - begin) // 2) as pair:
        for u in (begin, begin + 1):
            step(pair * 2 + u, u)
    for i in range(end, last):
        step(i, i)


def xattn_moe_kernel(nc, x, ctx_in, wqg, bqg, wkg, bkg, wvg, bvg, wql, bql, wkl, bkl, wvl, bvl, wp, bp,
                     gate_w, w1, b1, w2, b2, out):
    T, _, D = x.shape
    E, _, F = w1.shape
    C = D // P
    FC = F // P
    NH = 4
    HD = D // NH
    TOKENS = T * P
    NB = 2 * TOKENS // P + E - 1
    ROWS = TOKENS + P
    SCALE = float(D) ** -0.5
    XSCALE = 256.0
    WSCALE = 2.0 ** 14
    GROUPS = 4
    TG = T // GROUPS

    xn_dram = nc.dram_tensor("xn_rows", (ROWS, D + E), F32, kind="Internal").ap()
    acc_dram = nc.dram_tensor("acc_rows", (ROWS, D), F32, kind="Internal").ap()
    out_rows = out.rearrange("b s d -> (b s) d")

    with ExitStack() as ctx:
        def sb(name, shape, dt=F32):
            return ctx.enter_context(nc.sbuf_tensor(name, shape, dt))

        def sem(name):
            return ctx.enter_context(nc.semaphore(name))

        W1 = sb("W1", [P, E, C, 2, F], F16)
        W2 = sb("W2", [P, E, FC, D])
        W1in = W2[:, :, :, :].rearrange("p e c d -> p e (c d)")\
            .rearrange("p e (c f) -> p e c f", f=F)
        w1sq = sb("w1sq", [P, E, C])
        w1sum = sb("w1sum", [P, E])
        w1pow2 = sb("w1pow2", [P, E])
        w1scale = sb("w1scale", [P, E])
        h_unscale = sb("h_unscale", [P, E])
        X = sb("X", [P, T, D])
        XW = X[:, :, :].rearrange("p t d -> p (t d)").bitcast(F16)\
            .rearrange("p (n c r f) -> p n c r f", n=2, c=C, r=2)
        CX = sb("CX", [P, 2, NH, 2, HD])
        def carver(whole):
            used = [0]

            def piece(*shape):
                n = 1
                for s in shape:
                    n *= s
                a = whole[:, used[0]:used[0] + n]
                used[0] += n
                names = "abcd"[:len(shape)]
                return a.rearrange(f"p ({' '.join(names)}) -> p {' '.join(names)}", **dict(zip(names, shape)))

            return piece

        shared = sb("shared", [P, 30 * D])
        att = carver(shared)
        rout = carver(shared)
        exs = carver(shared)
        QW = att(2, D)
        QB = att(2, D)
        KW = att(2, D)
        KB = att(2, D)
        BP = att(D)
        ident = sb("ident", [P, P])
        ones = sb("ones", [P, P], BF16)
        ones32 = sb("ones32", [P, P])
        notri = sb("notri", [P, P], BF16)
        vrows = sb("vrows", [NH * 2 + C, P])
        vcols = sb("vcols", [P, NH * 2 + C])
        b2rows = sb("b2rows", [E, D])
        b2rest = sb("b2rest", [E, D])
        b2part = sb("b2part", [E, 3, D], BF16)
        b1rows = sb("b1rows", [E * FC, P])
        b1T = sb("b1T", [P, E * FC])
        GW = sb("GW", [P, C, E])
        half = sb("half", [P, 1])
        eps = sb("eps", [P, 1])
        st6 = sb("st6", [P, 2, 6])
        mv = sb("mv", [P, 2, 2, 2])
        rs = sb("rs", [P, 2, 2])
        qu = att(2, D)
        q = att(2, 2, D)
        k = att(2, 2, D)
        nmax = sb("nmax", [P, 2, 4])
        ex = att(2, 4, HD)
        pr = att(2, 4, HD)
        rsum = sb("rsum", [P, 2, 4])
        rinv = sb("rinv", [P, 2, 4])
        rw = sb("rw", [P, 2, 4])
        squares = att(F // 2)[:, :].bitcast(BF16)
        aT = att(C, P)
        vT = att(2, NH, P)
        xn = sb("xn", [P, 2, D])
        xnT = sb("xnT", [P, C, P])
        iotaE = sb("iotaE", [P, E])
        iotaB = sb("iotaB", [P, NB])
        iotaR = sb("iotaR", [P, P])
        iotaB128 = sb("iotaB128", [P, NB])
        tokid = sb("tokid", [P, T])
        slotno = sb("slotno", [P, 1])
        segm = sb("segm", [P, E, T])
        m12 = sb("m12", [P, 2, T])
        mask = rout(2, T * E)
        mk = [mask[:, n, :].rearrange("p (t e) -> p t e", e=E) for n in range(2)]
        tmpA = rout(T, E)
        tmpB = rout(T, E)
        tmpC = rout(E, T)
        tmpD = rout(E, T)
        picked = rout(2, T * E)
        chosen = sb("chosen", [P, E * T], BF16)
        comb = rout(T, E)
        combB = rout(T, E)
        sel = rout(T)
        ew = rout(T)
        den = rout(T)
        wk2 = sb("wk2", [P, 2, T])
        posf = sb("posf", [P, 2, T])
        posi = sb("posi", [P, 2, T], I32)
        slot_i = sb("slot_i", [P, 2, T], I32)
        blk_i = sb("blk_i", [P, 2, T], I32)
        slot_f = sb("slot_f", [P, 2, T])
        cnt_i = sb("cnt_i", [P, E], I32)
        cnt_blk = sb("cnt_blk", [P, E], I32)
        cslot = sb("cslot", [P, E])
        offs = sb("offs", [P, E])
        onesE = sb("onesE", [P, E])
        cmpb = rout(NB, E)
        ebf = sb("ebf", [P, NB])
        expert = sb("expert", [P, NB], I32)
        ohB = rout(2 * T, NB)
        V = rout(2 * T * NB // 2)[:, :].bitcast(F16).rearrange("p (t b) -> p t b", b=NB)
        ohR = rout(2 * T * P // 2)[:, :].bitcast(F16).rearrange("p (t s) -> p t s", s=P)
        tv = sb("tv", [P, NB])
        row_of = sb("row_of", [P, NB], I32)
        w_of = sb("w_of", [P, NB])
        gix = sb("gix", [P, 2], I32)
        six = sb("six", [P, 2], I32)
        XG = exs(2, D + E)
        XT = exs(2 * C * P)[:, :].bitcast(F16).rearrange("p (n r c t) -> p n r c t", n=2, r=2, c=C)
        hb = exs(FC, P)
        hT = exs(2, FC, P)
        Y = exs(2, D)
        B2 = sb("B2", [3, E, D], BF16)
        ones3 = sb("ones3", [3, P], BF16)

        ps = [ctx.enter_context(nc.psum_tensor(f"bank{n}", [P, 512], F32)) for n in range(8)]
        pS = [ps[n][:, 0:4 * HD].rearrange("p (c g e) -> p c g e", c=C, g=2) for n in range(2)]
        pCT = [ps[n][:, :].rearrange("p (h n) -> p h n", h=NH) for n in (2, 7)]
        pAT = ps[3][:, 0:D].rearrange("p (c d) -> p c d", c=C)
        pO = ps[4][:, 0:D]
        pXT = ps[5][:, 0:D].rearrange("p (c n) -> p c n", c=C)
        pL = ps[6][:, 0:T * E].rearrange("p (t e) -> p t e", e=E)
        pMisc = ps[6][:, T * E:3 * T * E]
        pB1 = ps[2][:, 0:E * FC]
        pTok = ps[7][:, 0:NB]
        pHT = [[ps[2 * n + m][:, :].rearrange("p (c n) -> p c n", n=P) for m in range(2)] for n in range(2)]
        pY = [ps[4][:, 0:D], ps[5][:, 0:D]]
        pGT = ps[6][:, 0:D].rearrange("p (c n) -> p c n", c=C)

        x_in = [sem(f"x_in{g}") for g in range(GROUPS)]
        c_in = [sem(f"c_in{n}") for n in range(2)]
        kc_in, qc_in, bp_in, v_in, w_in = sem("kc_in"), sem("qc_in"), sem("bp_in"), sem("v_in"), sem("w_in")
        b2_in, b2_cut, b2_placed = sem("b2_in"), sem("b2_cut"), sem("b2_placed")
        w1s_in = [sem(f"w1s_in{n}") for n in range(2)]
        zero_out = sem("zero_out")
        xn_out = [sem(f"xn_out{n}") for n in range(2)]
        x1_out = sem("x1_out")
        acc_in = [sem(f"acc_in{g}") for g in range(2 * GROUPS)]
        res_out = sem("res_out")
        made = sem("made")
        zeroed = sem("zeroed")
        kscaled = sem("kscaled")
        vtr, vcopied = sem("vtr"), sem("vcopied")
        w1_in = [sem(f"w1_in{n}") for n in range(2)]
        b1_in, gw_in, b1_tr, b1_ok = sem("b1_in"), sem("gw_in"), sem("b1_tr"), sem("b1_ok")
        sq_ok, sqsum_ok, wsum_ok, wpow_ok, scale_step, scale_ok = (
            sem("sq_ok"), sem("sqsum_ok"), sem("wsum_ok"), sem("wpow_ok"), sem("scale_step"), sem("scale_ok"))
        high_ok, low_ok = [sem(f"high_ok{c}") for c in range(C)], [sem(f"low_ok{c}") for c in range(C)]
        scaled_ok = sem("scaled_ok")
        high_late, scaled_late, low_late = sem("high_late"), sem("scaled_late"), sem("low_late")
        st1a, st1, rsa, rs_ok = sem("st1a"), sem("st1"), sem("rsa"), sem("rs_ok")
        qmul, q_ok, kmul, k_ok, xb_ok = sem("qmul"), sem("q_ok"), sem("kmul"), sem("k_ok"), sem("xb_ok")
        s_ok, max_ok, exp_ok, inv_ok, rw_ok, pr_ok = (sem("s_ok"), sem("max_ok"), sem("exp_ok"), sem("inv_ok"),
                                                      sem("rw_ok"), sem("pr_ok"))
        ct_ok, vt_ok, at_ok, as_ok, o_ok = sem("ct_ok"), sem("vt_ok"), sem("at_ok"), sem("as_ok"), sem("o_ok")
        x1_ok, st2a, st2, xn_ok = sem("x1_ok"), sem("st2a"), sem("st2"), sem("xn_ok")
        xt_ok, xts_ok, l_ok = sem("xt_ok"), sem("xts_ok"), sem("l_ok")
        waited_pool, waited_dve = sem("waited_pool"), sem("waited_dve")
        route = sem("route")
        gap_ok, gate_exp = sem("gap_ok"), sem("gate_exp")
        mask_ok, rank_ok = sem("mask_ok"), sem("rank_ok")
        expert_ok = sem("expert_ok")
        w_ok, ohb_ok, ohr_ok, table_mm, tok_ok = sem("w_ok"), sem("ohb_ok"), sem("ohr_ok"), sem("table_mm"), sem("tok_ok")
        comb_mul, comb_ok, comb_out, v_ok = sem("comb_mul"), sem("comb_ok"), sem("comb_out"), sem("v_ok")
        gix_ok, six_ok = sem("gix_ok"), sem("six_ok")
        xg_ok = [sem(f"xg_ok{n}") for n in range(2)]
        got_w, xh_ok = sem("got_w"), sem("xh_ok")
        gt_ok, gts_ok, h_ok, hb_ok, gelu_ok, y_ok, ys_ok, added = (
            sem("gt_ok"), sem("gts_ok"), sem("h_ok"), sem("hb_ok"), sem("gelu_ok"), sem("y_ok"), sem("ys_ok"),
            sem("added"))

        MADE = 15
        RS_FIRST = -3
        A_FIRST, A_LAST = -4, T + 4
        STEADY = (4, 10)
        B_LAST = NB + 2
        B_FROM, B_TO = 3, NB - 2
        B_TO -= (B_TO - B_FROM) % 2
        B_STEADY = (B_FROM, B_TO)

        def tile_on(i):
            return not isinstance(i, int) or 0 <= i < T

        SQ, SCALES = 4, 4 + E
        CUT = SCALES + 1
        LATE = E - 2

        def expert_on(i, u, start, experts=E):
            return start <= u < start + experts

        def block_on(i):
            return not isinstance(i, int) or 0 <= i < NB

        def group_loaded(eng, sems, t):
            if isinstance(t, int):
                eng.wait_ge(sems[t // TG], 16)
            else:
                for s in sems:
                    eng.wait_ge(s, 16)

        block = ctx.enter_context(nc.Block())

        @block.sync
        def _(sp):
            def load_group(dst, src, g, s):
                sp.dma_start(dst[:, g * TG:(g + 1) * TG, :],
                             src[g * TG:(g + 1) * TG].rearrange("t p d -> p t d")).then_inc(s, 16)

            def load_ctx(t, n):
                for r in range(2):
                    sp.dma_start(CX[:, n, :, r, :], ctx_in[bass.ds(t, 1)].rearrange("a p (h e) -> p (a h) e", e=HD))\
                      .then_inc(c_in[n], 16)

            load_group(X, x, 0, x_in[0])
            for dst, srcs in ((KW, (wkg, wkl)), (KB, (bkg, bkl))):
                for n, src in enumerate(srcs):
                    sp.dma_start(dst[:, n, :], src.partition_broadcast(P)).then_inc(kc_in, 16)
            load_ctx(0, 0)
            for r, (wv, bv) in enumerate(((wvg, bvg), (wvl, bvl))):
                for m, src in enumerate((wv, bv)):
                    sp.dma_start(vrows[m * NH:(m + 1) * NH, r * HD:(r + 1) * HD], src.rearrange("(h e) -> h e", e=HD))\
                      .then_inc(v_in, 16)
            sp.dma_start(vrows[2 * NH:2 * NH + C, :], wp.rearrange("(c p) -> c p", p=P)).then_inc(v_in, 16)
            load_ctx(1, 1)
            sp.dma_start(BP[:, :], bp.partition_broadcast(P)).then_inc(bp_in, 16)
            load_group(X, x, 1, x_in[1])
            sp.dma_start(b1rows[:, :], b1.rearrange("e (c p) -> (e c) p", p=P)).then_inc(b1_in, 16)
            sp.dma_start(GW[:, :, :], gate_w.rearrange("(c p) e -> p c e", p=P)).then_inc(gw_in, 16)
            for g in range(2, GROUPS):
                load_group(X, x, g, x_in[g])
            sp.dma_start(b2rows[:, :], b2).then_inc(b2_in, 16)
            sp.wait_ge(zeroed, 1)
            sp.dma_start(xn_dram[TOKENS:ROWS, :], pr.rearrange("p n a d -> p (n a d)")[:, 0:D + E]).then_inc(zero_out, 16)
            sp.dma_start(acc_dram[TOKENS:ROWS, :], pr[:, 0].rearrange("p a d -> p (a d)")).then_inc(zero_out, 16)

            def tiles(i, u):
                t = i + 4
                if tile_on(t) and not (isinstance(t, int) and t < 2):
                    sp.wait_ge(k_ok, t - 1)
                    sp.wait_ge(ct_ok, t - 1)
                    load_ctx(t, u % 2)
                t = i - 1
                if tile_on(t):
                    sp.wait_ge(x1_ok, t + 1)
                    sp.dma_start(acc_dram[bass.ds(t * P, P), :], X[:, bass.ds(t, 1), :].rearrange("p a d -> p (a d)"))\
                      .then_inc(x1_out, 16)
                t, n = i - 2, u % 2
                if tile_on(t):
                    sp.wait_ge(xn_ok, t + 1)
                    sp.dma_start(xn_dram[bass.ds(t * P, P), 0:D], xn[:, n, :]).then_inc(xn_out[n], 16)
                count = {-2: 2, -1: 2, 0: 2, 1: 2, 2: 1, 3: 1}
                if not isinstance(i, int):
                    chunks = [i + 6]
                elif i in count:
                    start = sum(n for k, n in count.items() if k < i)
                    chunks = range(start, start + count[i])
                else:
                    chunks = []
                for h in chunks:
                    c = h % 2 if isinstance(h, int) else u % 2
                    after(sp, w1_in[c], 8 * (h - c))
                    sp.dma_start(W1in[:, :, :, :].rearrange("p e c f -> p (e c) f")[:, bass.ds(h, 1), :]
                                 .rearrange("p a f -> p (a f)"),
                                 w1.rearrange("e (c p) f -> (e c) p f", p=P)[bass.ds(h, 1)]
                                 .rearrange("a p f -> p (a f)")).then_inc(w1_in[c], 16)
                e = i - (CUT + 2)
                if expert_on(i, u, CUT + 2, LATE):
                    sp.wait_ge(low_ok[0], e + 1)
                    sp.wait_ge(low_ok[1], e + 1)
                    sp.dma_start(W2[:, e], w2[e].rearrange("(c p) d -> p c d", p=P)).then_inc(w_in, 16)

            run_steps(sp, -4, CUT + 2 + LATE, STEADY, tiles)

            def load_w2_late(e):
                sp.wait_ge(low_late, C * (e + 1 - LATE))
                sp.dma_start(W2[:, e], w2[e].rearrange("(c p) d -> p c d", p=P)).then_inc(w_in, 16)

            for e in range(LATE, E):
                load_w2_late(e)

            def stage(b, n):
                if block_on(b):
                    e = sp.value_load(expert[0:1, bass.ds(b, 1)], min_val=0, max_val=E - 1)
                    after(sp, h_ok, 2 * (b - 1))
                    if isinstance(b, int) and b == 1:
                        sp.wait_ge(xg_ok[0], 16)
                    sp.dma_start(XW[:, n], W1[:, bass.ds(e, 1)].rearrange("p a c r f -> p (a c) r f"))\
                      .then_inc(w1s_in[n], 16)

            sp.wait_ge(expert_ok, 1)
            sp.wait_ge(x1_out, 16 * T)
            stage(0, 0)
            stage(1, 1)
            run_steps(sp, 2, NB, B_STEADY, lambda i, u: stage(i, u % 2))

            TH = TG // 2
            sp.wait_ge(added, 16 * NB)
            for g in range(2 * GROUPS):
                rows = slice(g * TH * P, (g + 1) * TH * P)
                sp.dma_start(X[:, g * TH:(g + 1) * TH, :], acc_dram[rows, :].rearrange("(t p) d -> p t d", p=P))\
                  .then_inc(acc_in[g], 16)
            sp.wait_ge(res_out, 16 * 2 * GROUPS)

        @block.gpsimd
        def _(pool):
            for dst, srcs in ((QW, (wqg, wql)), (QB, (bqg, bql))):
                for n, src in enumerate(srcs):
                    pool.dma_start(dst[:, n, :], src.partition_broadcast(P)).then_inc(qc_in, 16)
            pool.memset(pr, 0.0).then_inc(zeroed, 1)
            pool.memset(half[:, :], -0.5).then_inc(made, 1)
            pool.memset(eps[:, :], EPS).then_inc(made, 1)
            pool.memset(ident[:, :], 0.0).then_inc(made, 1)
            pool.memset(ones[:, :], 1.0).then_inc(made, 1)
            pool.memset(ones32[:, :], 1.0).then_inc(made, 1)
            pool.wait_ge(made, 5)
            pool.affine_select(out=ident[:, :], in_=ident[:, :], compare_op=ALU.not_equal, fill=1.0, base=0,
                               pattern=[[-1, P]], channel_multiplier=1).then_inc(made, 1)
            pool.memset(notri[:, :], 0.0).then_inc(zeroed, 1)
            pool.wait_ge(zeroed, 2)
            pool.affine_select(out=notri[:, :], in_=notri[:, :], compare_op=ALU.is_ge, fill=-1.0, base=-1,
                               pattern=[[1, P]], channel_multiplier=-1).then_inc(made, 1)
            pool.iota(iotaB128[:, :], pattern=[[P, NB]], base=0, channel_multiplier=0,
                      allow_small_or_imprecise_dtypes=True).then_inc(made, 1)
            pool.iota(iotaE[:, :], pattern=[[1, E]], base=-E, channel_multiplier=0,
                      allow_small_or_imprecise_dtypes=True).then_inc(made, 1)
            pool.iota(iotaB[:, :], pattern=[[1, NB]], base=0, channel_multiplier=0,
                      allow_small_or_imprecise_dtypes=True).then_inc(made, 1)
            pool.iota(iotaR[:, :], pattern=[[1, P]], base=0, channel_multiplier=0,
                      allow_small_or_imprecise_dtypes=True).then_inc(made, 1)
            pool.iota(tokid[:, :], pattern=[[P, T]], base=-TOKENS, channel_multiplier=1,
                      allow_small_or_imprecise_dtypes=True).then_inc(made, 1)
            pool.iota(slotno[:, :], pattern=[[0, 1]], base=0, channel_multiplier=1,
                      allow_small_or_imprecise_dtypes=True).then_inc(made, 1)
            pool.memset(onesE[:, :], 1.0).then_inc(made, 1)
            pool.memset(ones3[:, :], 1.0).then_inc(made, 1)
            pool.memset(segm[:, :, :], 1.0).then_inc(zeroed, 1)
            pool.wait_ge(zeroed, 3)
            pool.memset(segm[:, :, 0:1], 0.0).then_inc(zeroed, 1)

            def attention(i, u):
                t, t2, r = i + 3, i - 2, (u + 1) % 2
                if tile_on(t) or tile_on(t2):
                    ln = slice(0 if tile_on(t) else 1, 2 if tile_on(t2) else 1)
                    var, inv = mv[:, r, ln, 1:2], rs[:, r, ln].rearrange("p (l o) -> p l o", o=1)
                    cols = [P, ln.stop - ln.start, 1]
                    if tile_on(t):
                        after(pool, q_ok, t - 1)
                        pool.wait_ge(st1, t + 1)
                    if tile_on(t2):
                        after(pool, xn_ok, t2 - 1)
                        pool.wait_ge(st2, t2 + 1)
                    pool.tensor_tensor(inv, var, eps[:, :].rearrange("p (l o) -> p l o", o=1).broadcast_to(cols), ALU.add)\
                        .then_inc(rsa, 1)
                    pool.wait_ge(rsa, i + (1 - RS_FIRST))
                    pool.tensor_tensor(inv, inv, half[:, :].rearrange("p (l o) -> p l o", o=1).broadcast_to(cols), ALU.pow)\
                        .then_inc(rs_ok, 1)
                t, n = i + 2, u % 2
                if tile_on(t):
                    pool.wait_ge(c_in[n], 16 * (t - n) + 32)
                    pool.wait_ge(kscaled, 2)
                    after(pool, s_ok, t - 1)
                    c = CX[:, n].rearrange("p h g e -> p g h e")
                    pool.tensor_tensor(k[:, n].rearrange("p g (h e) -> p g h e", e=HD), c,
                                       KW.rearrange("p g (h e) -> p g h e", e=HD), ALU.mult).then_inc(kmul, 1)
                    pool.wait_ge(kmul, t + 1)
                    pool.tensor_tensor(k[:, n], k[:, n], KB[:, :, :], ALU.add).then_inc(k_ok, 1)
                t = i
                if tile_on(t):
                    xt = X[:, bass.ds(t, 1), :].rearrange("p a d -> p (a d)")
                    pool.wait_ge(q_ok, t + 1)
                    pool.wait_ge(bp_in, 16)
                    pool.tensor_tensor(xt, xt, BP[:, :], ALU.add).then_inc(xb_ok, 1)
                if u == SCALES:
                    pool.wait_ge(wsum_ok, 1)
                    pool.tensor_tensor(w1pow2[:, :], w1sum[:, :], half[:, :].broadcast_to([P, E]), ALU.pow).then_inc(wpow_ok, 1)

                if expert_on(i, u, CUT + 1, LATE):
                    e = i - (CUT + 1)
                    pool.wait_ge(scaled_ok, e + 1)
                    pool.tensor_tensor(W1[:, e, 1, 1, :], W1in[:, e, 1, :], W1[:, e, 1, 0, :], ALU.subtract)\
                        .then_inc(low_ok[1], 1)

            run_steps(pool, A_FIRST, A_LAST, STEADY, attention)

            for e in range(LATE, E):
                for c in range(C):
                    pool.wait_ge(scaled_late, C * (e - LATE) + (c + 1))
                    pool.tensor_tensor(W1[:, e, c, 1, :], W1in[:, e, c, :], W1[:, e, c, 0, :], ALU.subtract)\
                        .then_inc(low_late, 1)

            for n in range(2):
                pool.wait_ge(ohb_ok, 1)
                pool.tensor_tensor(V[:, n * T:(n + 1) * T, :], ohB[:, n * T:(n + 1) * T, :],
                                   tokid[:, :].rearrange("p (t o) -> p t o", o=1).broadcast_to([P, T, NB]), ALU.mult)\
                    .then_inc(v_ok, 1)

            pool.wait_ge(tok_ok, 1)
            pool.wait_ge(zero_out, 32)
            pool.wait_ge(comb_out, 16)
            pool.wait_ge(xn_out[0], 16 * (T // 2))

            def experts(i, u):
                b, n = i + 2, u % 2
                if block_on(b):
                    after(pool, xg_ok[n], 8 * (b - n))
                    pool.tensor_copy(gix[:, n:n + 1], row_of[:, bass.ds(b, 1)]).then_inc(gix_ok, 1)
                    pool.wait_ge(xn_out[1], 16 * (T // 2))
                    pool.wait_ge(gix_ok, b + 1)
                    after(pool, gt_ok, b - 1)
                    after(pool, got_w, b - 1)
                    pool.sem_inc(waited_pool, 1)
                    pool.indirect_dma_start(out=XG[:, n, :], out_offset=None, in_=xn_dram,
                                            in_offset=bass.IndirectOffsetOnAxis(ap=gix[:, n:n + 1], axis=0))\
                        .then_inc(xg_ok[n], 16)
                b, n = i - 2, u % 2
                if block_on(b):
                    after(pool, added, 16 * b)
                    pool.tensor_copy(six[:, n:n + 1], row_of[:, bass.ds(b, 1)]).then_inc(six_ok, 1)
                    pool.wait_ge(x1_out, 16 * T)
                    pool.wait_ge(six_ok, b + 1)
                    pool.wait_ge(ys_ok, b + 1)
                    pool.sem_inc(waited_pool, 1)
                    pool.indirect_dma_start(out=acc_dram,
                                            out_offset=bass.IndirectOffsetOnAxis(ap=six[:, n:n + 1], axis=0),
                                            in_=Y[:, n, :], in_offset=None, compute_op=ALU.add,
                                            bounds_check=ROWS - 1, oob_is_err=True).then_inc(added, 16)

            run_steps(pool, -2, B_LAST, B_STEADY, experts)

        @block.scalar
        def _(act):
            act.wait_ge(vtr, 1)
            act.activation(vcols[:, :], pMisc[:, 0:2 * NH + C], ACT.Copy).then_inc(vcopied, 1)
            act.wait_ge(vcopied, 1)
            act.activation(vcols[:, 2 * NH:], vcols[:, 2 * NH:], ACT.Copy, scale=2.0).then_inc(vcopied, 1)

            def attention(i, u):
                t = i - 1
                if tile_on(t):
                    act.wait_ge(at_ok, t + 1)
                    after(act, o_ok, t)
                    act.activation(aT, pAT, ACT.Copy).then_inc(as_ok, 1)
                t, n = i, u % 2
                if tile_on(t):
                    act.wait_ge(max_ok, t + 1)
                    after(act, pr_ok, t - 1)
                    for a in range(4):
                        act.activation(ex[:, n, a, :], pS[n][:, a // 2, a % 2, :], ACT.Exp, bias=nmax[:, n, a:a + 1],
                                       accum_out=rsum[:, n, a:a + 1]).then_inc(exp_ok, 1)
                e = i - SQ
                if expert_on(i, u, SQ):
                    for c in range(C):
                        act.wait_ge(w1_in[c], 16 * (e + 1))
                        after(act, sq_ok, C * e + c)
                        act.activation(squares, W1in[:, bass.ds(e, 1), c, :].rearrange("p a f -> p (a f)"), ACT.Square,
                                       accum_out=w1sq[:, bass.ds(e, 1), c]).then_inc(sq_ok, 1)
                if expert_on(i, u, CUT, LATE):
                    e = i - CUT
                    act.wait_ge(scale_ok, 2)
                    act.activation(W1[:, e, 0, 0, :], W1in[:, e, 0, :], ACT.Copy, scale=w1scale[:, e:e + 1])\
                       .then_inc(high_ok[0], 1)
                if expert_on(i, u, CUT + 1, LATE):
                    e = i - (CUT + 1)
                    act.wait_ge(high_ok[1], e + 1)
                    act.activation(W1in[:, e, 1, :], W1in[:, e, 1, :], ACT.Copy, scale=w1scale[:, e:e + 1])\
                       .then_inc(scaled_ok, 1)
                t = i - 3
                if tile_on(t):
                    act.wait_ge(xt_ok, t + 1)
                    after(act, l_ok, t)
                    act.activation(xnT[:, :, :], pXT, ACT.Copy).then_inc(xts_ok, 1)
                t, n = i + 1, (u + 1) % 2
                if tile_on(t):
                    act.wait_ge(ct_ok, t + 1)
                    after(act, o_ok, t - 1)
                    for h in range(NH):
                        act.activation(vT[:, n, h, :], pCT[n][:, h, :], ACT.Identity,
                                       bias=vcols[:, NH + h:NH + h + 1], scale=vcols[:, h:h + 1]).then_inc(vt_ok, 1)

            run_steps(act, A_FIRST, A_LAST, STEADY, attention)

            for e in range(LATE, E):
                for c in range(C):
                    act.activation(W1[:, e, c, 0, :], W1in[:, e, c, :], ACT.Copy, scale=w1scale[:, e:e + 1])\
                       .then_inc(high_late, 1)
                for c in range(C):
                    act.wait_ge(high_late, C * (e - LATE) + (c + 1))
                    act.activation(W1in[:, e, c, :], W1in[:, e, c, :], ACT.Copy, scale=w1scale[:, e:e + 1])\
                       .then_inc(scaled_late, 1)

            act.wait_ge(b1_tr, 1)
            act.activation(b1T[:, :], pB1, ACT.Copy).then_inc(b1_ok, 1)
            act.wait_ge(gap_ok, 1)
            act.activation(ew, sel, ACT.Exp).then_inc(gate_exp, 1)
            act.wait_ge(b2_cut, 5)
            for r in range(3):
                act.dma_start(B2[r:r + 1, :, :], b2part[:, r, :]).then_inc(b2_placed, 16)
            act.wait_ge(comb_ok, 1)
            act.dma_start(xn_dram[0:TOKENS, D:D + E].rearrange("(t p) e -> p t e", p=P), comb).then_inc(comb_out, 16)

            def experts(i, u):
                b, n = i + 1, (u + 1) % 2
                if block_on(b):
                    act.wait_ge(gt_ok, b + 1)
                    after(act, h_ok, 2 * (b - 1))
                    act.activation(XT[:, n, 0], pGT, ACT.Copy, scale=XSCALE).then_inc(xh_ok, 1)
                b, n = i, u % 2
                if block_on(b):
                    after(act, y_ok, b - 1)
                    for m in range(2):
                        act.wait_ge(hb_ok, 2 * b + (m + 1))
                        act.activation(hT[:, n, 4 * m:4 * m + 4, :], hb[:, 4 * m:4 * m + 4, :], ACT.Gelu)\
                           .then_inc(gelu_ok, 1)

            run_steps(act, -1, B_LAST, B_STEADY, experts)

            TH = TG // 2
            for g in range(2 * GROUPS):
                rows = slice(g * TH * P, (g + 1) * TH * P)
                act.wait_ge(acc_in[g], 16)
                act.dma_start(out_rows[rows, :].rearrange("(t p) d -> p t d", p=P), X[:, g * TH:(g + 1) * TH, :])\
                   .then_inc(res_out, 16)

        @block.vector
        def _(dve):
            def attention(i, u):
                t, n = i, u % 2
                if tile_on(t):
                    dve.wait_ge(s_ok, t + 1)
                    after(dve, exp_ok, 4 * (t - 1))
                    dve.tensor_reduce(nmax[:, n, :], pS[n].rearrange("p c g e -> p (c g) e"), AX.X, ALU.max,
                                      negate=True).then_inc(max_ok, 1)
                if u == A_FIRST + 2:
                    dve.wait_ge(kc_in, 16 * 4)
                    dve.tensor_scalar(KW[:, :, :], KW[:, :, :], SCALE, None, ALU.mult).then_inc(kscaled, 1)
                    dve.tensor_scalar(KB[:, :, :], KB[:, :, :], SCALE, None, ALU.mult).then_inc(kscaled, 1)
                tq, ts, n = i + 2, i + 4, u % 2
                if tile_on(tq):
                    xb = X[:, bass.ds(tq, 1), :].broadcast_to([P, 2, D])
                    dve.wait_ge(rs_ok, tq + 1)
                    dve.wait_ge(qc_in, 16 * 4)
                    after(dve, q_ok, tq)
                    dve.scalar_tensor_tensor(out=qu, in0=xb, scalar=mv[:, n, 0, 0:1], in1=QW,
                                             op0=ALU.subtract, op1=ALU.mult).then_inc(qmul, 1)
                if tile_on(ts):
                    group_loaded(dve, x_in, ts)
                    after(dve, st1, ts)
                    dve.sem_inc(waited_dve, 1)
                    dve.bn_stats(st6[:, 0, :], X[:, bass.ds(ts, 1), :].rearrange("p a d -> p (a d)")).then_inc(st1a, 1)
                if tile_on(tq):
                    after(dve, s_ok, tq - 1)
                    dve.wait_ge(qmul, tq + 1)
                    dve.scalar_tensor_tensor(out=q[:, n], in0=qu, scalar=rs[:, n, 0:1],
                                             in1=QB, op0=ALU.mult, op1=ALU.add).then_inc(q_ok, 1)
                if tile_on(ts):
                    dve.wait_ge(st1a, ts + 1)
                    after(dve, qmul, ts - 1)
                    after(dve, rsa, ts - 1)
                    dve.sem_inc(waited_dve, 1)
                    dve.bn_aggr(mv[:, n, 0, :], st6[:, 0, :]).then_inc(st1, 1)
                if u == SCALES:
                    dve.wait_ge(sqsum_ok, 1)
                    dve.tensor_scalar(w1sum[:, :], pMisc[:, 0:E], 1e-30, None, ALU.max).then_inc(wsum_ok, 1)
                if u == SCALES + 1:
                    dve.wait_ge(wpow_ok, 1)
                    power, undone = w1pow2[:, :].bitcast(I32), h_unscale[:, :].bitcast(I32)
                    dve.tensor_scalar(power, power, 0x7F800000, None, ALU.bitwise_and).then_inc(scale_step, 1)
                    dve.wait_ge(scale_step, 1)
                    dve.tensor_scalar(undone, power, -1.0, float(0x7F000000), ALU.mult, ALU.add).then_inc(scale_step, 1)
                    dve.tensor_scalar(w1scale[:, :], w1pow2[:, :], WSCALE, None, ALU.mult).then_inc(scale_ok, 1)
                    dve.wait_ge(scale_step, 2)
                    dve.tensor_scalar(h_unscale[:, :], h_unscale[:, :], 1.0 / (WSCALE * XSCALE), None, ALU.mult)\
                       .then_inc(scale_ok, 1)
                if expert_on(i, u, CUT, LATE):
                    e = i - CUT
                    dve.wait_ge(scale_ok, 2)
                    dve.tensor_scalar(W1[:, e, 1, 0, :], W1in[:, e, 1, :], w1scale[:, e:e + 1], None, ALU.mult)\
                       .then_inc(high_ok[1], 1)
                if expert_on(i, u, CUT + 1, LATE):
                    e = i - (CUT + 1)
                    dve.wait_ge(high_ok[0], e + 1)
                    dve.scalar_tensor_tensor(out=W1[:, e, 0, 1, :], in0=W1in[:, e, 0, :], scalar=w1scale[:, e:e + 1],
                                             in1=W1[:, e, 0, 0, :], op0=ALU.mult, op1=ALU.subtract).then_inc(low_ok[0], 1)
                t = i
                if tile_on(t):
                    dve.wait_ge(exp_ok, 4 * (t + 1))
                    dve.reciprocal(rinv[:, n, :], rsum[:, n, :]).then_inc(inv_ok, 1)
                tn = i - 2
                if tile_on(tn):
                    dve.wait_ge(rs_ok, tn + (3 - RS_FIRST))
                    after(dve, xn_out[n], 8 * (tn - n))
                    after(dve, xt_ok, tn - 1)
                    dve.tensor_scalar(xn[:, n, :], X[:, bass.ds(tn, 1), :].rearrange("p a d -> p (a d)"),
                                      mv[:, (u + 1) % 2, 1, 0:1], rs[:, (u + 1) % 2, 1:2], ALU.subtract, ALU.mult)\
                       .then_inc(xn_ok, 1)
                if tile_on(t):
                    dve.wait_ge(inv_ok, t + 1)
                    dve.wait_ge(vcopied, 2)
                    dve.tensor_tensor(rw[:, n, :].rearrange("p (c g) -> p c g", c=C),
                                      rinv[:, n, :].rearrange("p (c g) -> p c g", c=C),
                                      vcols[:, 2 * NH:].rearrange("p (c o) -> p c o", o=1).broadcast_to([P, C, 2]),
                                      ALU.mult).then_inc(rw_ok, 1)
                    dve.wait_ge(rw_ok, t + 1)
                    after(dve, at_ok, t - 1)
                    dve.wait_ge(zero_out, 32)
                    dve.tensor_tensor(pr[:, n], ex[:, n],
                                      rw[:, n, :].rearrange("p (a b) -> p a b", b=1).broadcast_to([P, 4, HD]),
                                      ALU.mult).then_inc(pr_ok, 1)
                t, n = i - 1, u % 2
                if tile_on(t):
                    xt = X[:, bass.ds(t, 1), :].rearrange("p a d -> p (a d)")
                    dve.wait_ge(xb_ok, t + 1)
                    dve.wait_ge(o_ok, t + 1)
                    dve.tensor_tensor(xt, pO, xt, ALU.add).then_inc(x1_ok, 1)
                    dve.wait_ge(x1_ok, t + 1)
                    after(dve, st2, t)
                    dve.sem_inc(waited_dve, 1)
                    dve.bn_stats(st6[:, 1, :], xt).then_inc(st2a, 1)
                    dve.wait_ge(st2a, t + 1)
                    after(dve, xn_ok, t - 1)
                    after(dve, rsa, t + (1 - RS_FIRST))
                    dve.sem_inc(waited_dve, 1)
                    dve.bn_aggr(mv[:, n, 1, :], st6[:, 1, :]).then_inc(st2, 1)
                if u == 0:
                    dve.wait_ge(b2_in, 16)
                    cuts = [0]

                    def cut(ins):
                        ins.then_inc(b2_cut, 1)
                        cuts[0] += 1
                        dve.wait_ge(b2_cut, cuts[0])

                    cut(dve.tensor_copy(b2part[:, 0, :], b2rows[:, :]))
                    cut(dve.tensor_tensor(b2rest[:, :], b2rows[:, :], b2part[:, 0, :], ALU.subtract))
                    cut(dve.tensor_copy(b2part[:, 1, :], b2rest[:, :]))
                    cut(dve.tensor_tensor(b2rest[:, :], b2rest[:, :], b2part[:, 1, :], ALU.subtract))
                    cut(dve.tensor_copy(b2part[:, 2, :], b2rest[:, :]))

            run_steps(dve, A_FIRST, A_LAST, STEADY, attention)

            steps = [0]

            def chain(ins):
                ins.then_inc(route, 1)
                steps[0] += 1
                dve.wait_ge(route, steps[0])

            def over_e(a):
                return a.rearrange("p (t o) -> p t o", o=1).broadcast_to([P, T, E])

            iota_te = iotaE[:, :].rearrange("p (o e) -> p o e", o=1).broadcast_to([P, T, E])
            dve.wait_ge(zeroed, 4)
            dve.wait_ge(l_ok, T)
            dve.wait_ge(made, MADE)
            logits = pL
            for n in range(2):
                best = m12[:, n, :]
                chain(dve.tensor_reduce(best, logits, AX.X, ALU.max))
                chain(dve.tensor_tensor(tmpA, logits, over_e(best), ALU.is_equal))
                chain(dve.tensor_tensor(tmpA, tmpA, iota_te, ALU.mult))
                chain(dve.tensor_reduce(sel, tmpA, AX.X, ALU.min))
                chain(dve.tensor_tensor(mk[n], iota_te, over_e(sel), ALU.is_equal))
                if n == 0:
                    chain(dve.scalar_tensor_tensor(out=tmpB, in0=mk[0], scalar=-BIG, in1=logits,
                                                   op0=ALU.mult, op1=ALU.add))
                    logits = tmpB
            dve.tensor_tensor(chosen[:, :].rearrange("p (e t) -> p t e", t=T), mk[0], mk[1], ALU.add).then_inc(mask_ok, 1)
            dve.tensor_tensor(sel, m12[:, 1, :], m12[:, 0, :], ALU.subtract).then_inc(gap_ok, 1)
            dve.wait_ge(rank_ok, 1)
            pBack = pMisc[:, 0:T * E].rearrange("p (e t) -> p e t", t=T)
            chain(dve.tensor_tensor_scan(tmpC.rearrange("p e t -> p (e t)"), segm[:, :, :].rearrange("p e t -> p (e t)"),
                                         pMisc[:, T * E:2 * T * E], 0.0, ALU.mult, ALU.add))
            last = tmpC[:, :, T - 1:T].rearrange("p e o -> p (e o)")
            chain(dve.tensor_scalar(cnt_i[:, :], last, float(P - 1), None, ALU.add))
            chain(dve.tensor_scalar(cnt_blk[:, :], cnt_i[:, :], -P, None, ALU.bitwise_and))
            chain(dve.tensor_tensor_scan(cslot[:, :], onesE[:, :], cnt_blk[:, :], 0.0, ALU.mult, ALU.add))
            chain(dve.tensor_tensor(offs[:, :], cslot[:, :], cnt_blk[:, :], ALU.subtract))
            chain(dve.tensor_tensor(tmpD, tmpC, offs[:, :].rearrange("p (e o) -> p e o", o=1).broadcast_to([P, E, T]),
                                    ALU.add))
            chain(dve.tensor_tensor(tmpA.rearrange("p t e -> p e t"), pBack, tmpD, ALU.add))
            chain(dve.tensor_tensor(picked, mask, tmpA.rearrange("p t e -> p (t e)").rearrange("p (o x) -> p o x", o=1)
                                    .broadcast_to([P, 2, T * E]), ALU.mult))
            chain(dve.tensor_reduce(posf[:, :, :].rearrange("p n t -> p (n t)"),
                                    picked.rearrange("p n (t e) -> p (n t) e", e=E), AX.X, ALU.add))
            chain(dve.tensor_copy(posi[:, :, :], posf[:, :, :]))
            dve.tensor_scalar(blk_i[:, :, :], posi[:, :, :], 7, None, ALU.arith_shift_right).then_inc(route, 1)
            dve.tensor_scalar(slot_i[:, :, :], posi[:, :, :], P - 1, None, ALU.bitwise_and).then_inc(route, 1)
            steps[0] += 2
            dve.wait_ge(route, steps[0])
            N2 = 2 * T
            dve.tensor_tensor(ohB, iotaB[:, :].rearrange("p (o b) -> p o b", o=1).broadcast_to([P, N2, NB]),
                              blk_i[:, :, :].rearrange("p n (t o) -> p (n t) o", o=1).broadcast_to([P, N2, NB]),
                              ALU.is_equal).then_inc(ohb_ok, 1)
            slots = slot_i[:, :, :].rearrange("p n (t o) -> p (n t) o", o=1)
            for h in range(N2 // 4):
                dve.tensor_tensor(ohR[:, 4 * h:4 * h + 4, :],
                                  iotaR[:, :].rearrange("p (o s) -> p o s", o=1).broadcast_to([P, 4, P]),
                                  slots[:, 4 * h:4 * h + 4].broadcast_to([P, 4, P]), ALU.is_equal).then_inc(ohr_ok, 1)
                if h == 0:
                    dve.wait_ge(gate_exp, 1)
                    chain(dve.tensor_scalar(den, ew, 1.0, None, ALU.add))
                    dve.reciprocal(wk2[:, 0, :], den).then_inc(w_ok, 1)
                    dve.wait_ge(w_ok, 1)
                    dve.tensor_tensor(wk2[:, 1, :], ew, wk2[:, 0, :], ALU.mult).then_inc(w_ok, 1)
                    dve.tensor_tensor(comb, mk[0], over_e(wk2[:, 0, :]), ALU.mult).then_inc(comb_mul, 1)
                    dve.wait_ge(w_ok, 2)
                    dve.tensor_tensor(combB, mk[1], over_e(wk2[:, 1, :]), ALU.mult).then_inc(comb_mul, 1)
                    dve.wait_ge(comb_mul, 2)
                    dve.tensor_tensor(comb, comb, combB, ALU.add).then_inc(comb_ok, 1)
                if h == 1:
                    chain(dve.tensor_tensor(cmpb, iotaB128[:, :].rearrange("p (b o) -> p b o", o=1)
                                            .broadcast_to([P, NB, E]),
                                            cslot[:, :].rearrange("p (o e) -> p o e", o=1).broadcast_to([P, NB, E]),
                                            ALU.is_ge))
                    chain(dve.tensor_reduce(ebf[:, :], cmpb, AX.X, ALU.add))
                    dve.tensor_scalar(expert[:, :], ebf[:, :], float(E - 1), None, ALU.min).then_inc(expert_ok, 1)
            dve.wait_ge(table_mm, N2)
            chain(dve.tensor_scalar(tv[:, :], pTok, 0.0, slotno[:, 0:1], ALU.is_ge, ALU.mult))
            dve.scalar_tensor_tensor(out=row_of[:, :], in0=pTok, scalar=float(TOKENS), in1=tv[:, :],
                                     op0=ALU.add, op1=ALU.add).then_inc(tok_ok, 1)
            dve.wait_ge(tok_ok, 1)
            dve.wait_ge(expert_ok, 1)
            dve.wait_ge(b1_ok, 1)

            def experts(i, u):
                b, n = i + 1, (u + 1) % 2
                if block_on(b):
                    dve.wait_ge(xh_ok, b + 1)
                    after(dve, h_ok, 2 * (b - 1))
                    dve.scalar_tensor_tensor(out=XT[:, n, 1], in0=pGT, scalar=XSCALE, in1=XT[:, n, 0],
                                             op0=ALU.mult, op1=ALU.subtract).then_inc(gts_ok, 1)
                    e = dve.value_load(expert[0:1, bass.ds(b, 1)], min_val=0, max_val=E - 1)
                    dve.wait_ge(xg_ok[n], 8 * (b + 2 - n))
                    dve.tensor_copy(w_of[:, bass.ds(b, 1)], XG[:, n, bass.ds(e + D, 1)]).then_inc(got_w, 1)
                b, n = i, u % 2
                if block_on(b):
                    e = dve.value_load(expert[0:1, bass.ds(b, 1)], min_val=0, max_val=E - 1)
                    for m in range(2):
                        dve.wait_ge(h_ok, 2 * b + (m + 1))
                        after(dve, gelu_ok, 2 * b + (m - 1))
                        dve.scalar_tensor_tensor(out=hb[:, 4 * m:4 * m + 4, :], in0=pHT[n][m],
                                                 scalar=h_unscale[:, bass.ds(e, 1)],
                                                 in1=b1T[:, bass.ds(e * FC + 4 * m, 4)]
                                                 .rearrange("p (c o) -> p c o", o=1).broadcast_to([P, 4, P]),
                                                 op0=ALU.mult, op1=ALU.add).then_inc(hb_ok, 1)
                b, n = i - 1, (u - 1) % 2
                if block_on(b):
                    dve.wait_ge(y_ok, b + 1)
                    after(dve, added, 16 * (b - 1))
                    dve.wait_ge(got_w, b + 1)
                    dve.tensor_scalar(Y[:, n, :], pY[n], w_of[:, bass.ds(b, 1)], None, ALU.mult).then_inc(ys_ok, 1)

            run_steps(dve, -1, B_LAST, B_STEADY, experts)

        @block.tensor
        def _(pe):
            pe.wait_ge(made, MADE)
            pe.wait_ge(v_in, 16 * 5)
            pe.transpose(pMisc[:, 0:2 * NH + C], vrows[:, :], ident[0:2 * NH + C, 0:2 * NH + C]).then_inc(vtr, 1)

            def attention(i, u):
                if u == SCALES:
                    pe.wait_ge(sq_ok, C * E)
                    for c in range(C):
                        mm = pe.matmul(pMisc[:, 0:E], ones32[:, :], w1sq[:, :, c], start=(c == 0), stop=(c == C - 1))
                    mm.then_inc(sqsum_ok, 1)
                t, n = i + 1, (u + 1) % 2
                if tile_on(t):
                    pe.wait_ge(q_ok, t + 1)
                    pe.wait_ge(k_ok, t + 1)
                    after(pe, exp_ok, 4 * (t - 1))
                    for c in range(C):
                        for g in range(2):
                            for h in range(2):
                                ch = slice(c * P + h * HD, c * P + (h + 1) * HD)
                                mm = pe.matmul(pS[n][h * HD:(h + 1) * HD, c, g, :], q[:, n, g, ch], k[:, n, g, ch],
                                               start=True, stop=True)
                    mm.then_inc(s_ok, 1)
                t, n = i + 2, u % 2
                if tile_on(t):
                    pe.wait_ge(c_in[n], 16 * (t - n) + 32)
                    after(pe, vt_ok, 4 * (t - 1))
                    for h in range(NH):
                        mm = pe.transpose(pCT[n][:, h, :],
                                          CX[:, n, h].rearrange("p g e -> p (g e)"), ident[:, :])
                    mm.then_inc(ct_ok, 1)
                t, n = i - 3, (u - 3) % 2
                if tile_on(t):
                    pe.wait_ge(xn_ok, t + 1)
                    after(pe, xts_ok, t)
                    for c in range(C):
                        mm = pe.transpose(pXT[:, c, :], xn[:, n, c * P:(c + 1) * P], ident[:, :])
                    mm.then_inc(xt_ok, 1)
                t, n = i - 1, (u - 1) % 2
                if tile_on(t):
                    pe.wait_ge(as_ok, t + 1)
                    pe.wait_ge(vt_ok, 4 * (t + 1))
                    after(pe, x1_ok, t)
                    for h in range(NH):
                        mm = pe.matmul(pO[:, h * HD:(h + 1) * HD], vT[:, n, h, :],
                                       aT[:, h // 2, (h % 2) * HD:(h % 2 + 1) * HD], start=True, stop=True)
                    mm.then_inc(o_ok, 1)
                if u == SCALES:
                    pe.wait_ge(wsum_ok, 1)
                t = i - 4
                if u == 4:
                    pe.wait_ge(gw_in, 16)
                if tile_on(t):
                    pe.wait_ge(xts_ok, t + 1)
                    for c in range(C):
                        mm = pe.matmul(pL[:, bass.ds(t, 1), :].rearrange("p a e -> p (a e)"), xnT[:, c, :], GW[:, c, :],
                                       start=(c == 0), stop=(c == C - 1))
                    mm.then_inc(l_ok, 1)
                t, n = i, u % 2
                if tile_on(t):
                    pe.wait_ge(pr_ok, t + 1)
                    after(pe, as_ok, t)
                    for c in range(C):
                        mm = pe.transpose(pAT[:, c, :], pr[:, n, 2 * c:2 * c + 2, :].rearrange("p g e -> p (g e)"),
                                          ident[:, :])
                    mm.then_inc(at_ok, 1)

            run_steps(pe, A_FIRST, A_LAST, STEADY, attention)

            pe.wait_ge(b1_in, 16)
            pe.transpose(pB1, b1rows[:, :], ident[0:E * FC, 0:E * FC]).then_inc(b1_tr, 1)
            pe.wait_ge(mask_ok, 1)
            pe.matmul(pMisc[:, 0:T * E], notri[:, :], chosen[:, :], start=True, stop=True)
            pe.matmul(pMisc[:, T * E:2 * T * E], ones[:, :], chosen[:, :], start=True, stop=True).then_inc(rank_ok, 1)

            for t in range(2 * T):
                pe.wait_ge(ohr_ok, t // 4 + 1)
                pe.wait_ge(v_ok, t // T + 1)
                pe.matmul(pTok, ohR[:, t, :], V[:, t, :], start=(t == 0), stop=(t == 2 * T - 1)).then_inc(table_mm, 1)

            pe.wait_ge(b2_placed, 16 * 3)
            pe.wait_ge(expert_ok, 1)
            pe.wait_ge(b1_ok, 1)

            def experts(i, u):
                b, n = i + 1, (u + 1) % 2
                if block_on(b):
                    pe.wait_ge(xg_ok[n], 8 * (b + 2 - n))
                    after(pe, gts_ok, b)
                    for c in range(C):
                        mm = pe.transpose(pGT[:, c, :], XG[:, n, c * P:(c + 1) * P], ident[:, :])
                    mm.then_inc(gt_ok, 1)
                b = i - 1
                if block_on(b):
                    e = pe.value_load(expert[0:1, bass.ds(b, 1)], min_val=0, max_val=E - 1)
                b, n = i, u % 2
                if block_on(b):
                    pe.wait_ge(w1s_in[n], 8 * (b + 2 - n))
                    pe.wait_ge(gts_ok, b + 1)
                    after(pe, hb_ok, 2 * (b - 1))
                    for m in range(2):
                        for f in range(4 * m, 4 * m + 4):
                            for c in range(C):
                                for w, x in ((0, 0), (0, 1), (1, 0)):
                                    mm = pe.matmul(pHT[n][m][:, f % 4, :], XW[:, n, c, w, f * P:(f + 1) * P],
                                                   XT[:, n, x, c, :], start=(c == 0 and w == 0 and x == 0),
                                                   stop=(c == C - 1 and w == 1))
                        mm.then_inc(h_ok, 1)
                b, n = i - 1, (u - 1) % 2
                if block_on(b):
                    if isinstance(b, int) and b == 0:
                        pe.wait_ge(w_in, 16 * E)
                    pe.wait_ge(gelu_ok, 2 * (b + 1))
                    after(pe, ys_ok, b - 1)
                    for f in range(FC):
                        pe.matmul(pY[n], hT[:, n, f, :], W2[:, bass.ds(e, 1), f, :].rearrange("p a d -> p (a d)"),
                                  start=(f == 0), stop=False)
                    pe.matmul(pY[n], ones3[:, :], B2[:, bass.ds(e, 1), :].rearrange("p a d -> p (a d)"),
                              start=False, stop=True).then_inc(y_ok, 1)

            run_steps(pe, -1, B_LAST, B_STEADY, experts)


_INS = ["x", "ctx_1024", "L0_xattn_wqg", "L0_xattn_bqg", "L0_xattn_wkg", "L0_xattn_bkg", "L0_xattn_wvg", "L0_xattn_bvg",
        "L0_xattn_wql", "L0_xattn_bql", "L0_xattn_wkl", "L0_xattn_bkl", "L0_xattn_wvl", "L0_xattn_bvl", "L0_xattn_wp",
        "L0_xattn_bp", "L0_ffn_gate_w", "L0_ffn_w1", "L0_ffn_b1", "L0_ffn_w2", "L0_ffn_b2"]


def kernel(**inputs):
    import numpy as _np
    import concourse.bacc as _bacc
    from concourse import mybir as _mybir
    from concourse.bass_utils import run_bass_kernel_spmd as _run

    nc = _bacc.Bacc("TRN2", target_bir_lowering=False, num_devices=1)
    arrays, args = {}, []
    for name in _INS:
        a = _np.ascontiguousarray(inputs[name])
        arrays[f"in_{name}"] = a
        args.append(nc.dram_tensor(f"in_{name}", a.shape, _mybir.dt.from_np(a.dtype), kind="ExternalInput").ap())
    args.append(nc.dram_tensor("out_0", inputs["x"].shape, _mybir.dt.float32, kind="ExternalOutput").ap())
    xattn_moe_kernel(nc, *args)
    r = _run(nc, [arrays], core_ids=[0])
    return r.results[0]["out_0"]
```
